# Optimizing a Trainium2 kernel written in Bass

```python
import numpy as np
import jax
import jax.numpy as jnp

def _softmax(x, axis=-1):
    return jax.nn.softmax(x, axis=axis)

def _gelu(x):
    return jax.nn.gelu(x, approximate=True)

def _silu(x):
    return jax.nn.silu(x)

def _sigmoid(x):
    return jax.nn.sigmoid(x)

def _layernorm(x, axis=-1, eps=1e-05):
    m = jnp.mean(x, axis=axis, keepdims=True)
    v = jnp.var(x, axis=axis, keepdims=True)
    return (x - m) / jnp.sqrt(v + eps)

def _scatter_add(tgt, idx, src, axis=0):
    return tgt.at[idx].add(src)

def _segment_sum(src, seg, n):
    return jax.ops.segment_sum(src, seg, n)
kernel_name = 'mk_adj_preln_d1_adj_r2_d87f23'

def setup_inputs(seed: int=0):
    np.random.seed(seed)
    _w = jnp.asarray

    def _rec_inputs():
        import jax
        import jax.numpy as jnp
        _gk = jax.random.key(seed)
        x = -0.0002928 + 1 * jax.random.normal(jax.random.fold_in(_gk, 1), (4096, 512), jnp.float32)
        _a = jax.random.bernoulli(jax.random.fold_in(_gk, 2), 0.000976562, (4096, 4096))
        _a = jnp.logical_or(_a, jnp.swapaxes(_a, -1, -2))
        _a = jnp.logical_or(_a, jnp.eye(4096, dtype=bool))
        _af = _a.astype(jnp.float32)
        adj = _af
        return (x, adj)
    x, adj = _rec_inputs()

    def _L0_gnn_setup():
        import jax, jax.numpy as jnp
        import numpy as np
        import math
        SENT_DIM = 512
        N_SENT = 2048
        key = jax.random.key(seed)
        ks = jax.random.split(key, 8)
        D = SENT_DIM
        s = 1.0 / math.sqrt(D)
        return {'sent_embed': jax.random.normal(ks[0], (N_SENT, D), dtype=jnp.float32), 'adj_tensor': jax.random.randint(ks[1], (N_SENT, N_SENT), 0, 2).astype(jnp.float32), 'W_q': jax.random.uniform(ks[2], (D, D), jnp.float32, -s, s), 'b_q': jax.random.uniform(ks[3], (D,), jnp.float32, -s, s), 'W_k': jax.random.uniform(ks[4], (D, D), jnp.float32, -s, s), 'b_k': jax.random.uniform(ks[5], (D,), jnp.float32, -s, s), 'W_v': jax.random.uniform(ks[6], (D, D), jnp.float32, -s, s), 'b_v': jax.random.uniform(ks[7], (D,), jnp.float32, -s, s)}
    _L0_gnn_all = _L0_gnn_setup()
    _L0_gnn_in = {k: v for k, v in _L0_gnn_all.items() if k in ('W_q', 'b_q', 'W_k', 'b_k', 'W_v', 'b_v')}
    del _L0_gnn_all
    return {'x': x, 'adj': adj, 'L0_gnn_W_q': _L0_gnn_in['W_q'], 'L0_gnn_b_q': _L0_gnn_in['b_q'], 'L0_gnn_W_k': _L0_gnn_in['W_k'], 'L0_gnn_b_k': _L0_gnn_in['b_k'], 'L0_gnn_W_v': _L0_gnn_in['W_v'], 'L0_gnn_b_v': _L0_gnn_in['b_v']}

def reference(x, adj, L0_gnn_W_q, L0_gnn_b_q, L0_gnn_W_k, L0_gnn_b_k, L0_gnn_W_v, L0_gnn_b_v):
    import jax
    import jax.numpy as jnp

    def _L0_gnn_ref(sent_embed, adj_tensor, W_q, b_q, W_k, b_k, W_v, b_v):
        import jax, jax.numpy as jnp
        import numpy as np
        import math
        SENT_DIM = 512
        N_SENT = 2048
        q = sent_embed @ W_q.T + b_q
        k = sent_embed @ W_k.T + b_k
        v = sent_embed @ W_v.T + b_v
        scale = 1.0 / math.sqrt(sent_embed.shape[-1])
        z = scale * (q @ k.T)
        spare_z = z * adj_tensor
        spare_z = jnp.where(spare_z == 0.0, jnp.asarray(-10000.0, spare_z.dtype), spare_z)
        attn = jax.nn.softmax(spare_z, axis=1)
        out = attn @ v
        return jax.nn.relu(out)
    h = jnp.maximum(_layernorm(x, axis=-1), 0.0)
    x = x + _L0_gnn_ref(h, adj, L0_gnn_W_q, L0_gnn_b_q, L0_gnn_W_k, L0_gnn_b_k, L0_gnn_W_v, L0_gnn_b_v)
    return x

_drawn_inputs = setup_inputs


def setup_inputs(seed=0):
    import zlib

    import numpy as np

    out = dict(_drawn_inputs(seed))
    spreads = {}
    factors = {'L0_gnn_W_q': 5.579,
     'L0_gnn_b_q': 8.0,
     'L0_gnn_W_k': 5.623,
     'L0_gnn_b_k': 8.0,
     'L0_gnn_b_v': 3.31}
    for name, (base, spread) in spreads.items():
        noise = np.random.default_rng([zlib.crc32(name.encode()), seed]).standard_normal(out[name].shape)
        drawn = base * np.exp(spread * noise) if base else spread * noise
        out[name] = jnp.asarray(drawn.astype(out[name].dtype))
    for name, factor in factors.items():
        out[name] = (out[name] * factor).astype(out[name].dtype)
    return out
```

```python
from contextlib import ExitStack

import concourse.bass as bass
from concourse import mybir

F32 = mybir.dt.float32
F16 = mybir.dt.float16
I32 = mybir.dt.int32
ALU = mybir.AluOpType
ACT = mybir.ActivationFunctionType
AX_X = mybir.AxisListType.X
ABSMAX = bass.bass_isa.ReduceOp.absmax

P = 128
NODES = 4096
DIM = 512
KC = DIM // P
TILES = NODES // P
CHUNK = 512
CHUNKS = NODES // CHUNK
BLOCKS = CHUNK // P
QUARTERS = 4
GROUP = 4
GROUPS = TILES // GROUP
EPS = 1e-5
SCALE = 1.0 / DIM ** 0.5
MASKED = -10000.0
LOWEST = -3.0e38
TINY = 1e-30
EXPONENT = 0x7F800000
HEADROOM = 16.0
P_SCALE = 16384.0


def adj_preln_attention(nc, x, adj, wq, bq, wk, bk, wv, bv, out):
    ctx = ExitStack()
    with ctx:
        def sb(name, shape, dt):
            return ctx.enter_context(nc.sbuf_tensor(name, shape, dt))

        def pb(name, shape, dt=F32):
            return ctx.enter_context(nc.psum_tensor(name, shape, dt))

        def sem(name):
            return ctx.enter_context(nc.semaphore(name))

        hT_hi = sb("hT_hi", [P, KC, NODES], F16)
        hT_lo = sb("hT_lo", [P, KC, NODES], F16)
        rows = sb("rows", [P, TILES, DIM], F32)
        v_pair = rows[:, :, :].bitcast(F16)
        ring = [sb(f"ring{u}", [P, NODES], F32) for u in range(2)]
        m_hi = sb("m_hi", [P, KC, DIM], F16)
        m_lo = sb("m_lo", [P, KC, DIM], F16)
        probs = [sb(f"probs{u}", [P, CHUNK], F32) for u in range(2)]
        pT_hi = [sb(f"pT_hi{u}", [P, BLOCKS, P], F16) for u in range(2)]
        pT_lo = [sb(f"pT_lo{u}", [P, BLOCKS, P], F16) for u in range(2)]
        penalty = [sb(f"penalty{u}", [P, CHUNK], F32) for u in range(2)]
        tT_hi = [sb(f"tT_hi{u}", [P, KC, P], F16) for u in range(2)]
        tT_lo = [sb(f"tT_lo{u}", [P, KC, P], F16) for u in range(2)]
        t_rows = sb("t_rows", [P, DIM], F32)
        u_all = sb("u_all", [P, DIM], F32)
        x_again = [sb(f"x_again{u}", [P, DIM], F32) for u in range(2)]
        o_rows = [sb(f"o_rows{u}", [P, DIM], F32) for u in range(2)]
        ident = sb("ident", [P, P], F32)
        s_all = sb("s_all", [P, TILES], F32)
        s_tile = [sb(f"s_tile{u}", [P, 1], F32) for u in range(2)]
        run_max = [sb(f"run_max{u}", [P, CHUNKS], F32) for u in range(2)]
        neg_max = [sb(f"neg_max{u}", [P, 1], F32) for u in range(2)]
        sums = [sb(f"sums{u}", [P, CHUNKS], F32) for u in range(2)]
        row_sum = sb("row_sum", [P, 1], F32)
        row_inv = sb("row_inv", [P, 1], F32)
        row_out = [sb(f"row_out{u}", [P, 1], F32) for u in range(2)]
        mag = [sb(f"mag{k}", [P, 4], F32) for k in range(2)]
        mag_all = [sb(f"mag_all{k}", [P, 4], F32) for k in range(2)]
        top = [sb(f"top{k}", [P, 1], F32) for k in range(2)]
        up = [sb(f"up{k}", [P, 1], F32) for k in range(2)]
        up_inv = [sb(f"up_inv{k}", [P, 1], F32) for k in range(2)]
        gain = sb("gain", [P, 1], F32)
        neg_gain = sb("neg_gain", [P, 1], F32)
        gain_inv = sb("gain_inv", [P, 1], F32)
        masked_at = sb("masked_at", [P, 1], F32)
        out_gain = sb("out_gain", [P, 1], F32)
        bq_bk = sb("bq_bk", [P, 1], F32)
        b_cols = sb("b_cols", [P, 2, KC], F32)
        zeros = sb("zeros", [P, P], F32)
        stats = sb("stats", [P, GROUP, 6], F32)
        mean_var = sb("mean_var", [P, GROUP, 2], F32)
        var_eps = sb("var_eps", [P, GROUP], F32)
        std = sb("std", [P, GROUP], F32)
        rstd = sb("rstd", [P, GROUP], F32)
        newton = sb("newton", [P, GROUP], F32)

        wq_sb = ring[1][:, 0:KC * DIM].rearrange("p (k n) -> p k n", k=KC)
        wk_sb = ring[1][:, KC * DIM:2 * KC * DIM].rearrange("p (k n) -> p k n", k=KC)
        m_f32 = ring[0][:, 0:KC * DIM].rearrange("p (k n) -> p k n", k=KC)
        wv_sb = ring[0][:, KC * DIM:2 * KC * DIM].rearrange("p (k n) -> p k n", k=KC)
        wvT_hi = sb("wvT_hi", [P, KC, DIM], F16)
        w_all = penalty[0]
        dot_waste = penalty[1]
        bv_all = t_rows
        b_wide = x_again[0][:, :].rearrange("p (k n) -> p k n", k=KC)
        bk_wide = x_again[1][:, :].rearrange("p (k n) -> p k n", k=KC)
        v_f32 = o_rows

        wvT_lo = sb("wvT_lo", [P, KC, DIM], F16)

        z_bank = [pb(f"z{u}", [P, CHUNK]) for u in range(2)]
        pT_bank = [pb(f"pT{u}", [P, BLOCKS, P]) for u in range(2)]
        o_bank = [pb(f"o{u}", [P, DIM]) for u in range(2)]
        t_bank = pb("t", [P, DIM])
        tT_bank = pb("tT", [P, KC, P])
        m_bank = [z_bank[0], z_bank[1], o_bank[0], o_bank[1]]
        wvT_bank = [pT_bank[0], pT_bank[1], t_bank[:, :].rearrange("p (k n) -> p k n", k=KC), tT_bank]
        hT_bank = pT_bank
        v_bank = z_bank

        names = """wv_loaded wqk_loaded bias_loaded bv_loaded x_loaded x_back_a x_back_b
            ident_zero ident_ready zeros_ready credits
            wvT_ready wide_ready m_ready bias_products_ready
            m_copied u_copied w_copied bqbk_copied mag_ready mag_reduced scale_seq scales_ready
            wvT_scaled_hi wvT_scaled_lo m_scaled_hi m_scaled_lo bv_scaled u_scaled
            stats_seq var_ready std_ready normed hT_ready hT_hi_ready hT_lo_ready dots_done
            v_ready v_summed v_hi_ready v_lo_ready s_all_ready
            t_ready t_copied tT_ready tT_hi_ready tT_lo_ready s_tile_ready
            z_ready scored penalised masked max_ready
            p_ready pT_ready pT_hi_ready pT_lo_ready o_ready pv_done
            sum_ready inv_ready row_out_ready relu_done added""".split()
        S = {n: sem(n) for n in names}
        adj_loaded = [[sem(f"adj_loaded{u}{q}") for q in range(QUARTERS)] for u in range(2)]
        x_back = [S["x_back_a"], S["x_back_b"]]
        stored = [sem("stored_a"), sem("stored_b")]

        class At:

            def __init__(self, half, u):
                self.half, self.u, self.n = half, u, half * 2 + u

            def back(self, k=1):
                d = self.u - k
                return At(self.half + d // 2, d % 2)

        def known(v):
            return isinstance(v, int)

        def after(eng, name, value):
            s = S[name] if isinstance(name, str) else name
            if not known(value) or value > 0:
                eng.wait_ge(s, value)

        def wide(ap3, n):
            if known(n):
                return ap3[:, :, n * P:(n + 1) * P]
            return ap3[:, :, bass.ds(n * P, P)]

        def cols(ap3, k, n):
            if known(n):
                return ap3[:, k, n * P:(n + 1) * P]
            return ap3[:, k, bass.ds(n * P, P)]

        def tile_of(ap3, n, a, b):
            if known(n):
                return ap3[:, n, a:b]
            return ap3[:, bass.ds(n, 1), a:b].rearrange("p o d -> p (o d)")

        block = ctx.enter_context(nc.Block())

        @block.sync
        def _(sp):
            sp.dma_start(wv_sb, wv.rearrange("(k p) n -> p k n", p=P)).then_inc(S["wv_loaded"], 16)
            sp.dma_start(bv_all[:, :], bv.rearrange("(o n) -> o n", o=1).partition_broadcast(P)
                         .rearrange("p o n -> p (o n)")).then_inc(S["bv_loaded"], 16)
            for j, b in enumerate((bq, bk)):
                sp.dma_start(b_cols[:, j, :], b.rearrange("(k p) -> p k", p=P),
                             allow_slow_non_contiguous=True).then_inc(S["bias_loaded"], 16)
            sp.dma_start(wq_sb, wq.rearrange("(k p) n -> p k n", p=P)).then_inc(S["wqk_loaded"], 16)
            sp.dma_start(wk_sb, wk.rearrange("(k p) n -> p k n", p=P)).then_inc(S["wqk_loaded"], 16)

            x_groups = x.rearrange("(g t p) d -> g p t d", t=GROUP, p=P)
            sp.dma_start(rows[:, 0:GROUP, :], x_groups[0]).then_inc(S["x_loaded"], 16)
            with sp.Fori(1, GROUPS) as g:
                first = sp.snap(g * GROUP)
                sp.wait_ge(S["x_loaded"], 16 * g)
                sp.dma_start(rows[:, bass.ds(first, GROUP), :],
                             x_groups[bass.ds(g, 1)].rearrange("o p t d -> (o p) t d")
                             ).then_inc(S["x_loaded"], 16)

            def start(n):
                return n * P if known(n) else sp.snap(n * P)

            def load_adj(at, row, q):
                w = NODES // QUARTERS
                sp.dma_start(ring[at.u][:, q * w:(q + 1) * w],
                             adj[bass.ds(row, P), q * w:(q + 1) * w]).then_inc(adj_loaded[at.u][q], 16)

            after(sp, "m_scaled_lo", 1)
            after(sp, "m_scaled_hi", 1)
            after(sp, "wvT_ready", KC)
            for q in range(QUARTERS):
                load_adj(At(0, 0), 0, q)

            def step(at, has_next=True, stores=True, prev=True, reload=True):
                row, row_back, row_next = start(at.n - 2), start(at.n - 1), start(at.n + 1)
                for q in range(QUARTERS):
                    if has_next:
                        if prev:
                            after(sp, "p_ready", CHUNKS * at.back().n + 2 * q + 2)
                        load_adj(at.back(-1), row_next, q)
                    if q == 1 and stores:
                        done = at.back(2)
                        after(sp, "added", done.n + 1)
                        sp.dma_start(out[bass.ds(row, P), :], o_rows[done.u][:, :]).then_inc(stored[done.u], 16)
                    if q == 2 and reload:
                        m = at.back()
                        after(sp, "added", m.n - 1)
                        sp.dma_start(x_again[m.u][:, :], x[bass.ds(row_back, P), :]).then_inc(x_back[m.u], 16)

            after(sp, "bias_products_ready", 1)
            step(At(0, 0), prev=False, stores=False, reload=False)
            step(At(0, 1), stores=False)
            step(At(1, 0))
            step(At(1, 1))
            with sp.Fori(2, TILES // 2 - 1) as i:
                step(At(i, 0))
                step(At(i, 1))
            last = TILES // 2 - 1
            step(At(last, 0))
            step(At(last, 1), has_next=False)
            step(At(last + 1, 0), has_next=False)
            step(At(last + 1, 1), has_next=False, reload=False)
            for u in range(2):
                sp.wait_ge(stored[u], 16 * (TILES // 2))

        @block.gpsimd
        def _(pool):
            nc.gpsimd.memset(ident[:, :], 0.0).then_inc(S["ident_zero"], 1)
            nc.gpsimd.memset(zeros[:, :], 0.0).then_inc(S["zeros_ready"], 1)
            pool.wait_ge(S["ident_zero"], 1)
            nc.gpsimd.affine_select(out=ident[:, :], in_=ident[:, :], compare_op=ALU.not_equal, fill=1.0,
                                    base=0, pattern=[[-1, P]], channel_multiplier=1
                                    ).then_inc(S["ident_ready"], 1)
            for k in range(2):
                after(pool, "mag_ready", k + 1)
                nc.gpsimd.partition_all_reduce(mag_all[k][:, :], mag[k][:, :], P, ABSMAX
                                               ).then_inc(S["mag_reduced"], 1)

            def v_low(at):
                after(pool, "v_hi_ready", at.n + 1)
                nc.gpsimd.tensor_tensor(tile_of(v_pair, at.n, DIM, 2 * DIM), v_f32[at.u][:, :],
                                        tile_of(v_pair, at.n, 0, DIM), ALU.subtract
                                        ).then_inc(S["v_lo_ready"], 1)

            with pool.Fori(0, TILES // 2) as i:
                v_low(At(i, 0))
                v_low(At(i, 1))

            def add_x(at):
                after(pool, "relu_done", at.n + 1)
                after(pool, x_back[at.u], 16 * at.half + 16)
                nc.gpsimd.tensor_tensor(o_rows[at.u][:, :], o_rows[at.u][:, :], x_again[at.u][:, :],
                                        ALU.add).then_inc(S["added"], 1)

            with pool.Fori(0, TILES // 2) as i:
                add_x(At(i, 0))
                add_x(At(i, 1))

        @block.tensor
        def _(pe):
            pe.wait_ge(S["ident_ready"], 1)
            pe.wait_ge(S["wv_loaded"], 16)
            for k in range(KC):
                for e in range(KC):
                    mm = pe.transpose(wvT_bank[k][:, e, :], wv_sb[:, e, k * P:(k + 1) * P], ident[:, :])
                mm.then_inc(S["wvT_ready"], 1)
            pe.wait_ge(S["wqk_loaded"], 32)
            for d in range(KC):
                for e in range(KC):
                    mm = pe.matmul(m_bank[d][:, :], wq_sb[:, e, d * P:(d + 1) * P], wk_sb[:, e, :],
                                   start=(e == 0), stop=(e == KC - 1))
                mm.then_inc(S["m_ready"], 1)
            pe.wait_ge(S["wide_ready"], 8)
            after(pe, "wvT_scaled_lo", KC)
            after(pe, "wvT_scaled_hi", KC)
            for dst, lhs, rhs in ((wvT_bank[2], b_wide, wk_sb), (wvT_bank[3], bk_wide, wq_sb)):
                for e in range(KC):
                    pe.matmul(dst.rearrange("p k n -> p (k n)") if dst is wvT_bank[2] else
                              dst[:, :, :].rearrange("p k n -> p (k n)"), lhs[:, e, :], rhs[:, e, :],
                              start=(e == 0), stop=(e == KC - 1))
            for e in range(KC):
                mm = pe.matmul(pT_bank[0][:, 0, 0:1], bk_wide[:, e, :], b_cols[:, 0, e:e + 1],
                               start=(e == 0), stop=(e == KC - 1))
            mm.then_inc(S["bias_products_ready"], 1)

            def transpose_h(at):
                after(pe, "normed", at.n + 1)
                after(pe, "hT_lo_ready", at.n - 1)
                for k in range(KC):
                    mm = pe.transpose(hT_bank[at.u][:, k, :], tile_of(rows, at.n, k * P, (k + 1) * P),
                                      ident[:, :])
                mm.then_inc(S["hT_ready"], 1)

            def project_v(at):
                after(pe, "hT_lo_ready", at.n + 1)
                after(pe, "v_summed", at.n - 1)
                for k in range(KC):
                    for j, (a, b) in enumerate(((hT_hi, wvT_hi), (hT_hi, wvT_lo), (hT_lo, wvT_hi))):
                        mm = pe.matmul(v_bank[at.u][:, :], cols(a, k, at.n), b[:, k, :],
                                       start=(k == 0 and j == 0), stop=(k == KC - 1 and j == 2))
                mm.then_inc(S["v_ready"], 1)

            after(pe, "bqbk_copied", 1)
            after(pe, "m_copied", KC)
            for n in range(TILES):
                transpose_h(At(n // 2, n % 2))
                if n:
                    project_v(At((n - 1) // 2, (n - 1) % 2))
            project_v(At(TILES // 2 - 1, 1))

            def fold_t(at):
                after(pe, "tT_hi_ready", at.n)
                for k in range(KC):
                    for j, (a, b) in enumerate(((hT_hi, m_hi), (hT_hi, m_lo), (hT_lo, m_hi))):
                        mm = pe.matmul(t_bank[:, :], cols(a, k, at.n), b[:, k, :],
                                       start=(k == 0 and j == 0), stop=(k == KC - 1 and j == 2))
                mm.then_inc(S["t_ready"], 1)

            def transpose_t(at):
                after(pe, "t_copied", at.n + 1)
                after(pe, "tT_lo_ready", at.n)
                for k in range(KC):
                    mm = pe.transpose(tT_bank[:, k, :], t_rows[:, k * P:(k + 1) * P], ident[:, :])
                mm.then_inc(S["tT_ready"], 1)

            def scores(at, c):
                if c == 0:
                    after(pe, "tT_lo_ready", at.n + 1)
                after(pe, "scored", CHUNKS * at.n + c - 1)
                span = slice(c * CHUNK, (c + 1) * CHUNK)
                for k in range(KC):
                    for j, (a, b) in enumerate(((tT_hi, hT_hi), (tT_hi, hT_lo), (tT_lo, hT_hi))):
                        mm = pe.matmul(z_bank[c % 2][:, :], a[at.u][:, k, :], b[:, k, span],
                                       start=(k == 0 and j == 0), stop=(k == KC - 1 and j == 2))
                mm.then_inc(S["z_ready"], 1)

            def transpose_p(at, c):
                after(pe, "p_ready", CHUNKS * at.n + c + 1)
                after(pe, "pT_lo_ready", CHUNKS * at.n + c - 1)
                for b in range(BLOCKS):
                    mm = pe.transpose(pT_bank[c % 2][:, b, :], probs[c % 2][:, b * P:(b + 1) * P], ident[:, :])
                mm.then_inc(S["pT_ready"], 1)

            def weigh_v(at, c):
                if c == 0:
                    after(pe, "relu_done", at.n - 1)
                after(pe, "pT_lo_ready", CHUNKS * at.n + c + 1)
                for b in range(BLOCKS):
                    j = c * BLOCKS + b
                    for s, (a, off) in enumerate(((pT_hi, 0), (pT_hi, DIM), (pT_lo, 0))):
                        mm = pe.matmul(o_bank[at.u][:, :], a[c % 2][:, b, :], v_pair[:, j, off:off + DIM],
                                       start=(c == 0 and b == 0 and s == 0),
                                       stop=(c == CHUNKS - 1 and b == BLOCKS - 1 and s == 2))
                mm.then_inc(S["pv_done"], 1)

            def step(at, own=True, prev=True, older=True, fold=True):
                for c in range(CHUNKS):
                    if own:
                        scores(at, c)
                    if prev:
                        transpose_p(at.back(), c)
                    if c == 0 and older:
                        weigh_v(at.back(2), CHUNKS - 1)
                    if c > 0 and prev:
                        weigh_v(at.back(), c - 1)
                    if c == 2 and fold:
                        fold_t(at.back(-1))
                    if c == 3 and fold:
                        transpose_t(at.back(-1))

            after(pe, "w_copied", 1)
            after(pe, "u_copied", 1)
            after(pe, "m_scaled_lo", 1)
            after(pe, "m_scaled_hi", 1)
            fold_t(At(0, 0))
            transpose_t(At(0, 0))
            after(pe, "v_lo_ready", TILES)
            step(At(0, 0), prev=False, older=False)
            step(At(0, 1), older=False)
            with pe.Fori(1, TILES // 2 - 1) as i:
                step(At(i, 0))
                step(At(i, 1))
            last = TILES // 2 - 1
            step(At(last, 0))
            step(At(last, 1), fold=False)
            step(At(last + 1, 0), own=False, fold=False)
            weigh_v(At(last, 1), CHUNKS - 1)

        @block.scalar
        def _(act):
            def flat(ap3):
                return ap3.rearrange("p k n -> p (k n)")

            for d in range(KC):
                after(act, "m_ready", d + 1)
                nc.scalar.copy(m_f32[:, d, :], m_bank[d][:, :]).then_inc(S["m_copied"], 1)
            after(act, "scales_ready", 1)
            for k in range(KC):
                b = wvT_bank[k] if k == 2 else wvT_bank[k][:, :, :]
                nc.scalar.activation(wvT_hi[:, k, :], flat(b), ACT.Copy, scale=up[0][:, 0:1]
                                     ).then_inc(S["wvT_scaled_hi"], 1)

            def root(g):
                after(act, "var_ready", g + 1)
                nc.scalar.activation(std[:, :], var_eps[:, :], ACT.Sqrt).then_inc(S["std_ready"], 1)

            def high_h(at):
                after(act, "hT_ready", at.n + 1)
                nc.scalar.activation(wide(hT_hi, at.n), hT_bank[at.u][:, :, :], ACT.Relu
                                     ).then_inc(S["hT_hi_ready"], 1)

            def high_v(at):
                after(act, "v_summed", at.n + 1)
                nc.scalar.copy(tile_of(v_pair, at.n, 0, DIM), v_f32[at.u][:, :]).then_inc(S["v_hi_ready"], 1)

            for n in range(TILES):
                if n % GROUP == 0 and n == 0:
                    root(0)
                high_h(At(n // 2, n % 2))
                if n == 0:
                    after(act, "scales_ready", 2)
                    nc.scalar.activation(flat(m_hi[:, :, :]), flat(m_f32), ACT.Copy, scale=up[1][:, 0:1]
                                         ).then_inc(S["m_scaled_hi"], 1)
                if n:
                    high_v(At((n - 1) // 2, (n - 1) % 2))
                if n % GROUP == GROUP - 2 and n // GROUP + 1 < GROUPS:
                    root(n // GROUP + 1)
            high_v(At(TILES // 2 - 1, 1))

            def high_t(at):
                after(act, "tT_ready", at.n + 1)
                nc.scalar.copy(tT_hi[at.u][:, :, :], tT_bank[:, :, :]).then_inc(S["tT_hi_ready"], 1)

            def exp(at, c):
                if c == 0:
                    after(act, "max_ready", at.n + 1)
                after(act, "pT_ready", CHUNKS * at.n + c - 1)
                nc.scalar.activation(probs[c % 2][:, :], ring[at.u][:, c * CHUNK:(c + 1) * CHUNK], ACT.Exp,
                                     bias=neg_max[at.u][:, 0:1], scale=gain[:, 0:1],
                                     accum_out=sums[at.u][:, c:c + 1]).then_inc(S["p_ready"], 1)

            def high_p(at, c):
                after(act, "pT_ready", CHUNKS * at.n + c + 1)
                after(act, "pv_done", CHUNKS * at.n + c - 1)
                nc.scalar.mul(pT_hi[c % 2][:, :, :], pT_bank[c % 2][:, :, :], P_SCALE
                              ).then_inc(S["pT_hi_ready"], 1)

            def relu_out(at):
                after(act, "pv_done", CHUNKS * at.n + CHUNKS)
                after(act, "row_out_ready", at.n + 1)
                after(act, stored[at.u], 16 * at.half)
                nc.scalar.activation(o_rows[at.u][:, :], o_bank[at.u][:, :], ACT.Relu,
                                     scale=row_out[at.u][:, 0:1]).then_inc(S["relu_done"], 1)

            def step(at, prev=True, older=True, fold=True):
                for c in range(CHUNKS):
                    if c == 4 and fold:
                        high_t(at.back(-1))
                    if prev:
                        exp(at.back(), c)
                    if c == 1 and older:
                        relu_out(at.back(2))
                    if prev:
                        high_p(at.back(), c)

            high_t(At(0, 0))
            after(act, "v_lo_ready", TILES)
            step(At(0, 0), prev=False, older=False)
            step(At(0, 1), older=False)
            step(At(1, 0))
            step(At(1, 1))
            with act.Fori(2, TILES // 2 - 1) as i:
                step(At(i, 0))
                step(At(i, 1))
            last = TILES // 2 - 1
            step(At(last, 0))
            step(At(last, 1), fold=False)
            step(At(last + 1, 0), fold=False)
            relu_out(At(last, 1))

        @block.vector
        def _(dve):
            v = nc.vector
            seq = [0]

            def link(ins):
                seq[0] += 1
                ins.then_inc(S["scale_seq"], 1)
                dve.wait_ge(S["scale_seq"], seq[0])

            def flat(ap3):
                return ap3.rearrange("p k n -> p (k n)")

            def magnitude(k):
                after(dve, "mag_reduced", k + 1)
                link(v.tensor_reduce(top[k][:, :], mag_all[k][:, :], AX_X, ALU.max))
                link(v.tensor_scalar(top[k][:, :], top[k][:, :], TINY, None, ALU.max))
                link(v.tensor_scalar(up_inv[k][:, :].bitcast(I32), top[k][:, :].bitcast(I32), EXPONENT, None,
                                     ALU.bitwise_and))
                link(v.tensor_scalar(up_inv[k][:, :], up_inv[k][:, :], 1.0 / HEADROOM, None, ALU.mult))
                v.reciprocal(up[k][:, :], up_inv[k][:, :]).then_inc(S["scales_ready"], 1)
                after(dve, "scales_ready", k + 1)

            dve.wait_ge(S["zeros_ready"], 1)
            dve.wait_ge(S["bias_loaded"], 32)
            for j, w in enumerate((b_wide, bk_wide)):
                for k in range(KC):
                    v.tensor_scalar(w[:, k, :], zeros[:, :], b_cols[:, j, k:k + 1], None, ALU.add
                                    ).then_inc(S["wide_ready"], 1)
            dve.wait_ge(S["wv_loaded"], 16)
            dve.wait_ge(S["bv_loaded"], 16)
            v.tensor_reduce(mag[0][:, 0:1], flat(wv_sb), AX_X, ALU.max)
            v.tensor_reduce(mag[0][:, 1:2], flat(wv_sb), AX_X, ALU.min)
            v.tensor_reduce(mag[0][:, 2:3], bv_all[:, :], AX_X, ALU.max)
            link(v.tensor_reduce(mag[0][:, 3:4], bv_all[:, :], AX_X, ALU.min))
            v.tensor_scalar(mag[0][:, 2:4], mag[0][:, 2:4], 1.0 / DIM, None, ALU.mult
                            ).then_inc(S["mag_ready"], 1)
            magnitude(0)
            v.tensor_scalar(bv_all[:, :], bv_all[:, :], up[0][:, 0:1], None, ALU.mult
                            ).then_inc(S["bv_scaled"], 1)
            v.tensor_scalar(out_gain[:, :], up_inv[0][:, :], 1.0 / P_SCALE, None, ALU.mult)
            for k in range(KC):
                after(dve, "wvT_scaled_hi", k + 1)
                b = wvT_bank[k] if k == 2 else wvT_bank[k][:, :, :]
                v.scalar_tensor_tensor(out=wvT_lo[:, k, :], in0=flat(b), scalar=up[0][:, 0:1],
                                       in1=wvT_hi[:, k, :], op0=ALU.mult, op1=ALU.subtract
                                       ).then_inc(S["wvT_scaled_lo"], 1)
            dve.wait_ge(S["bias_products_ready"], 1)
            v.tensor_copy(w_all[:, :], flat(tT_bank[:, :, :])).then_inc(S["w_copied"], 1)
            v.tensor_copy(bq_bk[:, :], pT_bank[0][:, 0, 0:1]).then_inc(S["bqbk_copied"], 1)
            v.tensor_copy(u_all[:, :], t_bank[:, :]).then_inc(S["u_copied"], 1)
            dve.wait_ge(S["u_copied"], 1)
            after(dve, "m_copied", KC)
            v.tensor_reduce(mag[1][:, 0:1], flat(m_f32), AX_X, ALU.max)
            v.tensor_reduce(mag[1][:, 1:2], flat(m_f32), AX_X, ALU.min)
            v.tensor_reduce(mag[1][:, 2:3], u_all[:, :], AX_X, ALU.max)
            link(v.tensor_reduce(mag[1][:, 3:4], u_all[:, :], AX_X, ALU.min))
            v.tensor_scalar(mag[1][:, 2:4], mag[1][:, 2:4], 1.0 / DIM, None, ALU.mult
                            ).then_inc(S["mag_ready"], 1)

            STATS = 6

            def row_stats(g):
                after(dve, "x_loaded", 16 * g + 16)
                for j in range(GROUP):
                    ins = v.bn_stats(stats[:, j, :], tile_of(rows, g * GROUP + j, 0, DIM))
                ins.then_inc(S["stats_seq"], 1)
                after(dve, "stats_seq", STATS * g + 1)
                for j in range(GROUP):
                    ins = v.bn_aggr(mean_var[:, j, :], stats[:, j, :])
                ins.then_inc(S["stats_seq"], 1)
                after(dve, "stats_seq", STATS * g + 2)
                v.tensor_scalar(var_eps[:, :], mean_var[:, :, 1], EPS, None, ALU.add
                                ).then_inc(S["var_ready"], 1)

            def row_rstd(g):
                after(dve, "std_ready", g + 1)
                v.reciprocal(rstd[:, :], std[:, :]).then_inc(S["stats_seq"], 1)
                after(dve, "stats_seq", STATS * g + 3)
                v.tensor_tensor(newton[:, :], rstd[:, :], rstd[:, :], ALU.mult).then_inc(S["stats_seq"], 1)
                after(dve, "stats_seq", STATS * g + 4)
                v.scalar_tensor_tensor(out=newton[:, :], in0=newton[:, :], scalar=-0.5, in1=var_eps[:, :],
                                       op0=ALU.mult, op1=ALU.mult).then_inc(S["stats_seq"], 1)
                after(dve, "stats_seq", STATS * g + 5)
                v.scalar_tensor_tensor(out=rstd[:, :], in0=newton[:, :], scalar=1.5, in1=rstd[:, :],
                                       op0=ALU.add, op1=ALU.mult).then_inc(S["stats_seq"], 1)
                after(dve, "stats_seq", STATS * g + 6)

            def normalise(g):
                for j in range(GROUP):
                    r = tile_of(rows, g * GROUP + j, 0, DIM)
                    v.tensor_scalar(r, r, mean_var[:, j, 0:1], rstd[:, j:j + 1], ALU.subtract, ALU.mult
                                    ).then_inc(S["normed"], 1)

            def row_dot(at):
                after(dve, "normed", at.n + 1)
                v.scalar_tensor_tensor(out=dot_waste[:, :], in0=tile_of(rows, at.n, 0, DIM), scalar=0.0,
                                       in1=w_all[:, :], op0=ALU.max, op1=ALU.mult,
                                       accum_out=s_all[:, at.n:at.n + 1]).then_inc(S["dots_done"], 1)

            def low_h(at):
                after(dve, "hT_hi_ready", at.n + 1)
                v.scalar_tensor_tensor(out=wide(hT_lo, at.n), in0=hT_bank[at.u][:, :, :], scalar=0.0,
                                       in1=wide(hT_hi, at.n), op0=ALU.max, op1=ALU.subtract
                                       ).then_inc(S["hT_lo_ready"], 1)

            def sum_v(at):
                after(dve, "v_ready", at.n + 1)
                after(dve, "v_lo_ready", at.n - 1)
                v.tensor_tensor(v_f32[at.u][:, :], v_bank[at.u][:, :], bv_all[:, :], ALU.add
                                ).then_inc(S["v_summed"], 1)

            dve.wait_ge(S["bv_scaled"], 1)
            dve.wait_ge(S["w_copied"], 1)
            row_stats(0)
            row_rstd(0)
            for n in range(TILES):
                g = n // GROUP
                if n % GROUP == 0:
                    normalise(g)
                low_h(At(n // 2, n % 2))
                row_dot(At(n // 2, n % 2))
                if n:
                    sum_v(At((n - 1) // 2, (n - 1) % 2))
                if n % GROUP == GROUP - 2 and g + 1 < GROUPS:
                    row_stats(g + 1)
                if n % GROUP == GROUP - 1 and g + 1 < GROUPS:
                    row_rstd(g + 1)
                if n == 0:
                    magnitude(1)
                    link(v.tensor_scalar(gain[:, :], up_inv[1][:, :], SCALE, None, ALU.mult))
                    v.tensor_scalar(neg_gain[:, :], gain[:, :], -1.0, None, ALU.mult)
                    link(v.reciprocal(gain_inv[:, :], gain[:, :]))
                    v.tensor_scalar(masked_at[:, :], gain_inv[:, :], MASKED, None, ALU.mult)
                    v.tensor_scalar(u_all[:, :], u_all[:, :], up[1][:, 0:1], None, ALU.mult
                                    ).then_inc(S["u_scaled"], 1)
                if n == 1:
                    after(dve, "m_scaled_hi", 1)
                    v.scalar_tensor_tensor(out=flat(m_lo[:, :, :]), in0=flat(m_f32), scalar=up[1][:, 0:1],
                                           in1=flat(m_hi[:, :, :]), op0=ALU.mult, op1=ALU.subtract
                                           ).then_inc(S["m_scaled_lo"], 1)
            sum_v(At(TILES // 2 - 1, 1))
            after(dve, "dots_done", TILES)
            v.tensor_scalar(s_all[:, :], s_all[:, :], bq_bk[:, 0:1], up[1][:, 0:1], ALU.add, ALU.mult
                            ).then_inc(S["s_all_ready"], 1)
            dve.wait_ge(S["s_all_ready"], 1)
            dve.wait_ge(S["u_scaled"], 1)

            def copy_t(at):
                after(dve, "t_ready", at.n + 1)
                after(dve, "tT_ready", at.n)
                v.tensor_tensor(t_rows[:, :], t_bank[:, :], u_all[:, :], ALU.add).then_inc(S["t_copied"], 1)
                col = s_all[:, at.n:at.n + 1] if known(at.n) else s_all[:, bass.ds(at.n, 1)]
                v.tensor_copy(s_tile[at.u][:, :], col).then_inc(S["s_tile_ready"], 1)

            def low_t(at):
                after(dve, "tT_hi_ready", at.n + 1)
                v.tensor_tensor(tT_lo[at.u][:, :, :], tT_bank[:, :, :], tT_hi[at.u][:, :, :], ALU.subtract
                                ).then_inc(S["tT_lo_ready"], 1)

            def mask(at, c):
                g = CHUNKS * at.n + c
                part = ring[at.u][:, c * CHUNK:(c + 1) * CHUNK]
                after(dve, "z_ready", g + 1)
                if c == 0:
                    after(dve, "s_tile_ready", at.n + 1)
                if c % 2 == 0:
                    after(dve, adj_loaded[at.u][c // 2], 16 * at.half + 16)
                v.scalar_tensor_tensor(out=part, in0=z_bank[c % 2][:, :], scalar=s_tile[at.u][:, 0:1], in1=part,
                                       op0=ALU.add, op1=ALU.mult).then_inc(S["scored"], 1)
                after(dve, "scored", g + 1)
                v.tensor_scalar(penalty[c % 2][:, :], part, 0.0, masked_at[:, 0:1], ALU.is_equal, ALU.mult
                                ).then_inc(S["penalised"], 1)
                after(dve, "scales_ready", 2)
                after(dve, "penalised", g + 1)
                start = LOWEST if c == 0 else run_max[at.u][:, c - 1:c]
                if c:
                    after(dve, "masked", g)
                v.tensor_tensor_reduce(out=part, in0=part, in1=penalty[c % 2][:, :], scale=1.0, scalar=start,
                                       op0=ALU.add, op1=ALU.max, accum_out=run_max[at.u][:, c:c + 1]
                                       ).then_inc(S["masked"], 1)

            def finish_max(at):
                after(dve, "masked", CHUNKS * at.n + CHUNKS)
                v.tensor_scalar(neg_max[at.u][:, :], run_max[at.u][:, CHUNKS - 1:CHUNKS], neg_gain[:, 0:1], None,
                                ALU.mult).then_inc(S["max_ready"], 1)

            def low_p(at, c):
                after(dve, "pT_hi_ready", CHUNKS * at.n + c + 1)
                v.scalar_tensor_tensor(out=pT_lo[c % 2][:, :, :], in0=pT_bank[c % 2][:, :, :], scalar=P_SCALE,
                                       in1=pT_hi[c % 2][:, :, :], op0=ALU.mult, op1=ALU.subtract
                                       ).then_inc(S["pT_lo_ready"], 1)

            def row_gain(at):
                after(dve, "p_ready", CHUNKS * at.n + CHUNKS)
                v.tensor_reduce(row_sum[:, :], sums[at.u][:, :], AX_X, ALU.add).then_inc(S["sum_ready"], 1)
                after(dve, "sum_ready", at.n + 1)
                v.reciprocal(row_inv[:, :], row_sum[:, :]).then_inc(S["inv_ready"], 1)
                after(dve, "inv_ready", at.n + 1)
                v.tensor_tensor(row_out[at.u][:, :], row_inv[:, :], out_gain[:, :], ALU.mult
                                ).then_inc(S["row_out_ready"], 1)

            def step(at, own=True, prev=True, fold=True):
                for c in range(CHUNKS):
                    if c == 3 and fold:
                        copy_t(at.back(-1))
                    if own:
                        mask(at, c)
                        if c == CHUNKS - 1:
                            finish_max(at)
                    if prev:
                        low_p(at.back(), c)
                    if c == 4 and fold:
                        low_t(at.back(-1))
                if prev:
                    row_gain(at.back())

            copy_t(At(0, 0))
            low_t(At(0, 0))
            step(At(0, 0), prev=False)
            step(At(0, 1))
            with dve.Fori(1, TILES // 2 - 1) as i:
                step(At(i, 0))
                step(At(i, 1))
            last = TILES // 2 - 1
            step(At(last, 0))
            step(At(last, 1), fold=False)
            step(At(last + 1, 0), own=False, fold=False)


_INS = ["x", "adj", "L0_gnn_W_q", "L0_gnn_b_q", "L0_gnn_W_k", "L0_gnn_b_k", "L0_gnn_W_v", "L0_gnn_b_v"]


def kernel(**inputs):
    import numpy as _np
    import concourse.bacc as _bacc
    from concourse import mybir as _mybir
    from concourse.bass_utils import run_bass_kernel_spmd as _run

    nc = _bacc.Bacc("TRN2", target_bir_lowering=False, num_devices=1)
    arrays, args = {}, []
    for name in _INS:
        a = _np.ascontiguousarray(inputs[name])
        arrays[f"in_{name}"] = a
        args.append(nc.dram_tensor(f"in_{name}", a.shape, _mybir.dt.from_np(a.dtype), kind="ExternalInput").ap())
    out = nc.dram_tensor("out", (NODES, DIM), F32, kind="ExternalOutput").ap()
    adj_preln_attention(nc, *args, out)
    r = _run(nc, [arrays], core_ids=[0])
    return r.results[0]["out"]
```

```python
from contextlib import ExitStack

import concourse.bass as bass
from concourse import mybir

F32 = mybir.dt.float32
F16 = mybir.dt.float16
I32 = mybir.dt.int32
U32 = mybir.dt.uint32
ALU = mybir.AluOpType
ACT = mybir.ActivationFunctionType
AX_X = mybir.AxisListType.X
ABSMAX = bass.bass_isa.ReduceOp.absmax

P = 128
NODES = 4096
DIM = 512
KC = DIM // P
TILES = NODES // P
CHUNK = 512
CHUNKS = NODES // CHUNK
BLOCKS = CHUNK // P
SQ = 32
QUADS = P // SQ
QUARTERS = 4
GROUP = 4
GROUPS = TILES // GROUP
EPS = 1e-5
SCALE = 1.0 / DIM ** 0.5
MASKED = -10000.0
LOWEST = -3.0e38
TINY = 1e-30
EXPONENT = 0x7F800000
HEADROOM = 16.0
P_SCALE = 16384.0


def adj_preln_attention(nc, x, adj, wq, bq, wk, bk, wv, bv, out):
    ctx = ExitStack()
    with ctx:
        def sb(name, shape, dt):
            return ctx.enter_context(nc.sbuf_tensor(name, shape, dt))

        def pb(name, shape, dt=F32):
            return ctx.enter_context(nc.psum_tensor(name, shape, dt))

        def sem(name):
            return ctx.enter_context(nc.semaphore(name))

        hT_hi = sb("hT_hi", [P, KC, NODES], F16)
        hT_lo = sb("hT_lo", [P, KC, NODES], F16)
        rows = sb("rows", [P, TILES, DIM], F32)
        v_pair = rows[:, :, :].bitcast(F16)
        ring = [sb(f"ring{u}", [P, NODES], F32) for u in range(2)]
        m_hi = sb("m_hi", [P, KC, DIM], F16)
        m_lo = sb("m_lo", [P, KC, DIM], F16)
        p_pair = [sb(f"p_pair{u}", [P, CHUNK, 2], F16) for u in range(2)]
        p_turned = [sb(f"p_turned{u}", [P, CHUNK, 2], F16) for u in range(2)]
        pT_pair = [sb(f"pT_pair{u}", [P, BLOCKS, P, 2], F16) for u in range(2)]
        penalty = [sb(f"penalty{u}", [P, CHUNK], F32) for u in range(2)]
        tT_hi = [sb(f"tT_hi{u}", [P, KC, P], F16) for u in range(2)]
        tT_lo = [sb(f"tT_lo{u}", [P, KC, P], F16) for u in range(2)]
        t_rows = sb("t_rows", [P, DIM], F32)
        u_all = sb("u_all", [P, DIM], F32)
        x_again = sb("x_again", [P, DIM], F32)
        o_rows = sb("o_rows", [P, DIM], F32)
        ident = sb("ident", [P, P], F32)
        s_all = sb("s_all", [P, TILES], F32)
        s_tile = [sb(f"s_tile{u}", [P, 1], F32) for u in range(2)]
        run_max = [sb(f"run_max{u}", [P, CHUNKS], F32) for u in range(2)]
        neg_max = [sb(f"neg_max{u}", [P, 1], F32) for u in range(2)]
        sums = [sb(f"sums{u}", [P, CHUNKS], F32) for u in range(2)]
        bv_all = sb("bv_all", [P, DIM], F32)
        row_sum = sb("row_sum", [P, 1], F32)
        row_inv = sb("row_inv", [P, 1], F32)
        row_out = [sb(f"row_out{u}", [P, 1], F32) for u in range(2)]
        mag_v = sb("mag_v", [P, KC], F32)
        mag_m = sb("mag_m", [P, KC + 1], F32)
        mag = [mag_v, mag_m]
        mag_all = [sb("mag_all_v", [P, KC], F32), sb("mag_all_m", [P, KC + 1], F32)]
        top = [sb(f"top{k}", [P, 1], F32) for k in range(2)]
        up = [sb(f"up{k}", [P, 1], F32) for k in range(2)]
        up_inv = [sb(f"up_inv{k}", [P, 1], F32) for k in range(2)]
        gain = sb("gain", [P, 1], F32)
        neg_gain = sb("neg_gain", [P, 1], F32)
        gain_inv = sb("gain_inv", [P, 1], F32)
        masked_at = sb("masked_at", [P, 1], F32)
        out_gain = sb("out_gain", [P, 1], F32)
        bq_bk = sb("bq_bk", [P, 1], F32)
        b_cols = sb("b_cols", [P, 2, KC], F32)
        zeros = sb("zeros", [P, P], F32)
        stats = sb("stats", [P, GROUP, 6], F32)
        mean_var = sb("mean_var", [P, GROUP, 2], F32)
        mean = sb("mean", [P, TILES], F32)
        var_eps = sb("var_eps", [P, TILES], F32)
        root = sb("root", [P, TILES], F32)
        rstd = sb("rstd", [P, TILES], F32)
        newton = sb("newton", [P, GROUP], F32)

        half = KC * DIM
        wv_sb = ring[0][:, 0:half].rearrange("p (k n) -> p k n", k=KC)
        wk_sb = ring[0][:, half:2 * half].rearrange("p (k n) -> p k n", k=KC)
        wq_sb = ring[1][:, 0:half].rearrange("p (k n) -> p k n", k=KC)
        wvT = ring[1][:, half:2 * half].bitcast(F16).rearrange("p (s k n) -> p s k n", s=2, k=KC)
        wvT_hi, wvT_lo = wvT[:, 0], wvT[:, 1]
        m_f32 = rows[:, TILES - GROUP:TILES, :]
        w_all = penalty[0]
        dot_waste = penalty[1]
        def as_rows(pair):
            return pair[:, :, :].rearrange("p c s -> p (c s)").bitcast(F32)

        b_wide, bk_wide = (as_rows(b).rearrange("p (k n) -> p k n", k=KC) for b in p_turned)
        normal = [as_rows(b) for b in p_turned]
        v_f32 = [as_rows(b) for b in p_pair]

        z_bank = [pb(f"z{u}", [P, CHUNK]) for u in range(2)]
        p_bank = [pb(f"p{u}", [P, CHUNK]) for u in range(2)]
        o_bank = [pb(f"o{u}", [P, DIM]) for u in range(2)]
        t_bank = pb("t", [P, DIM])
        tT_bank = pb("tT", [P, KC, P])
        hT_bank = [b[:, :].rearrange("p (k n) -> p k n", k=KC) for b in p_bank]
        wvT_bank = hT_bank + [t_bank[:, :].rearrange("p (k n) -> p k n", k=KC), tT_bank[:, :, :]]
        u_bank, w_bank, bq_bk_bank = o_bank[0][:, :], o_bank[1][:, :], z_bank[0][:, 0:1]
        m_bank = [z_bank[1][:, :], t_bank[:, :], tT_bank[:, :, :].rearrange("p k n -> p (k n)"), o_bank[0][:, :]]
        v_bank = z_bank

        wv_loaded = sem("wv_loaded")
        wqk_loaded = sem("wqk_loaded")
        bias_loaded = sem("bias_loaded")
        bv_loaded = sem("bv_loaded")
        x_loaded = sem("x_loaded")
        x_back = sem("x_back")
        stored = sem("stored")
        ident_zero = sem("ident_zero")
        ident_ready = sem("ident_ready")
        zeros_ready = sem("zeros_ready")
        wvT_ready = sem("wvT_ready")
        wide_ready = sem("wide_ready")
        m_ready = sem("m_ready")
        bias_products_ready = sem("bias_products_ready")
        m_copied = sem("m_copied")
        u_copied = sem("u_copied")
        w_copied = sem("w_copied")
        bqbk_copied = sem("bqbk_copied")
        mag_ready = sem("mag_ready")
        mag_reduced = sem("mag_reduced")
        scale_seq = sem("scale_seq")
        scales_ready = sem("scales_ready")
        wvT_scaled_hi = sem("wvT_scaled_hi")
        wvT_scaled_lo = sem("wvT_scaled_lo")
        m_scaled_hi = sem("m_scaled_hi")
        m_scaled_lo = sem("m_scaled_lo")
        u_scaled = sem("u_scaled")
        stats_ready = sem("stats_ready")
        aggregated = sem("aggregated")
        var_ready = sem("var_ready")
        root_ready = sem("root_ready")
        inv_root = sem("inv_root")
        newton_seq = sem("newton_seq")
        rstd_ready = sem("rstd_ready")
        normed = sem("normed")
        hT_ready = sem("hT_ready")
        hT_hi_ready = sem("hT_hi_ready")
        hT_lo_ready = sem("hT_lo_ready")
        dots_done = sem("dots_done")
        v_ready = sem("v_ready")
        v_copied = sem("v_copied")
        v_lo_ready = sem("v_lo_ready")
        s_all_ready = sem("s_all_ready")
        t_ready = sem("t_ready")
        t_copied = sem("t_copied")
        tT_ready = sem("tT_ready")
        tT_hi_ready = sem("tT_hi_ready")
        tT_lo_ready = sem("tT_lo_ready")
        s_tile_ready = sem("s_tile_ready")
        z_ready = sem("z_ready")
        scored = sem("scored")
        penalised = sem("penalised")
        masked = sem("masked")
        max_ready = sem("max_ready")
        p_ready = sem("p_ready")
        p_hi_ready = sem("p_hi_ready")
        p_lo_ready = sem("p_lo_ready")
        turned = sem("turned")
        moved_by_vector = sem("moved_by_vector")
        moved_by_scalar = sem("moved_by_scalar")
        pv_done = sem("pv_done")
        sum_ready = sem("sum_ready")
        inv_ready = sem("inv_ready")
        row_out_ready = sem("row_out_ready")
        o_scaled = sem("o_scaled")
        finished = sem("finished")
        adj_loaded = [[sem(f"adj_loaded{u}{q}") for q in range(QUARTERS)] for u in range(2)]
        class At:

            def __init__(self, half, u):
                self.half, self.u, self.n = half, u, half * 2 + u

            def back(self, k=1):
                d = self.u - k
                return At(self.half + d // 2, d % 2)

        def known(v):
            return isinstance(v, int)

        def tile_in(g, j):
            return At(g * (GROUP // 2) + j // 2, j % 2)

        def due(count):
            return not known(count) or count > 0

        def wide(ap3, n):
            if known(n):
                return ap3[:, :, n * P:(n + 1) * P]
            return ap3[:, :, bass.ds(n * P, P)]

        def cols(ap3, k, n):
            if known(n):
                return ap3[:, k, n * P:(n + 1) * P]
            return ap3[:, k, bass.ds(n * P, P)]

        def tile_of(ap3, n, a, b):
            if known(n):
                return ap3[:, n, a:b]
            return ap3[:, bass.ds(n, 1), a:b].rearrange("p o d -> p (o d)")

        def quadrant_moves(copy, u, targets):
            for p in targets:
                for q in range(QUADS):
                    src = p_turned[u][q * SQ:(q + 1) * SQ, :, :].rearrange(
                        "c (m b a) s -> c m b (a s)", m=BLOCKS, b=QUADS)[:, :, p, :]
                    dst = pT_pair[u][p * SQ:(p + 1) * SQ, :, q * SQ:(q + 1) * SQ, :].rearrange(
                        "c m a s -> c m (a s)")
                    ins = copy(dst, src)
            return ins

        block = ctx.enter_context(nc.Block())

        @block.sync
        def _(sp):
            sp.dma_start(wv_sb, wv.rearrange("(k p) n -> p k n", p=P)).then_inc(wv_loaded, 16)
            sp.dma_start(bv_all[:, :], bv.rearrange("(o n) -> o n", o=1).partition_broadcast(P)
                         .rearrange("p o n -> p (o n)")).then_inc(bv_loaded, 16)
            for j, b in enumerate((bq, bk)):
                sp.dma_start(b_cols[:, j, :], b.rearrange("(k p) -> p k", p=P),
                             allow_slow_non_contiguous=True).then_inc(bias_loaded, 16)
            sp.dma_start(wq_sb, wq.rearrange("(k p) n -> p k n", p=P)).then_inc(wqk_loaded, 16)
            sp.dma_start(wk_sb, wk.rearrange("(k p) n -> p k n", p=P)).then_inc(wqk_loaded, 16)

            x_groups = x.rearrange("(g t p) d -> g p t d", t=GROUP, p=P)
            sp.dma_start(rows[:, 0:GROUP, :], x_groups[0]).then_inc(x_loaded, 16)
            with sp.Fori(1, GROUPS - 1) as g:
                first = sp.snap(g * GROUP)
                sp.wait_ge(x_loaded, 16 * g)
                sp.dma_start(rows[:, bass.ds(first, GROUP), :],
                             x_groups[bass.ds(g, 1)].rearrange("o p t d -> (o p) t d")
                             ).then_inc(x_loaded, 16)

            sp.wait_ge(x_loaded, 16 * (GROUPS - 1))
            sp.wait_ge(m_scaled_lo, KC)
            sp.dma_start(rows[:, TILES - GROUP:TILES, :], x_groups[GROUPS - 1]).then_inc(x_loaded, 16)

            def start(n):
                return n * P if known(n) else sp.snap(n * P)

            def load_adj(at, row, q):
                w = NODES // QUARTERS
                sp.dma_start(ring[at.u][:, q * w:(q + 1) * w],
                             adj[bass.ds(row, P), q * w:(q + 1) * w]).then_inc(adj_loaded[at.u][q], 16)

            for q in range(QUARTERS):
                load_adj(At(0, 0), 0, q)

            def step(at, has_next=True, stores=True, prev=True, reload=True):
                row, row_back, row_next = start(at.n - 2), start(at.n - 1), start(at.n + 1)
                for q in range(QUARTERS):
                    if has_next:
                        if prev:
                            sp.wait_ge(p_ready, CHUNKS * at.back().n + 2 * q + 2)
                        load_adj(at.back(-1), row_next, q)
                    if q == 1 and stores:
                        done = at.back(2)
                        sp.wait_ge(finished, done.n + 1)
                        sp.dma_start(out[bass.ds(row, P), :], o_rows[:, :]).then_inc(stored, 16)
                    if q == 2 and reload:
                        m = at.back()
                        if due(m.n):
                            sp.wait_ge(finished, m.n)
                        sp.dma_start(x_again[:, :], x[bass.ds(row_back, P), :]).then_inc(x_back, 16)

            sp.wait_ge(v_ready, TILES)
            step(At(0, 0), prev=False, stores=False, reload=False)
            step(At(0, 1), stores=False)
            step(At(1, 0))
            step(At(1, 1))
            with sp.Fori(2, TILES // 2 - 1) as i:
                step(At(i, 0))
                step(At(i, 1))
            last = TILES // 2 - 1
            step(At(last, 0))
            step(At(last, 1), has_next=False)
            step(At(last + 1, 0), has_next=False)
            step(At(last + 1, 1), has_next=False, reload=False)
            sp.wait_ge(stored, 16 * TILES)

        @block.gpsimd
        def _(pool):
            nc.gpsimd.memset(ident[:, :], 0.0).then_inc(ident_zero, 1)
            nc.gpsimd.memset(zeros[:, :], 0.0).then_inc(zeros_ready, 1)
            pool.wait_ge(ident_zero, 1)
            nc.gpsimd.affine_select(out=ident[:, :], in_=ident[:, :], compare_op=ALU.not_equal, fill=1.0,
                                    base=0, pattern=[[-1, P]], channel_multiplier=1
                                    ).then_inc(ident_ready, 1)
            for k in range(2):
                pool.wait_ge(mag_ready, k + 1)
                nc.gpsimd.partition_all_reduce(mag_all[k][:, :], mag[k][:, :], P, ABSMAX
                                               ).then_inc(mag_reduced, 1)

            def low_v(at):
                pool.wait_ge(v_copied, at.n + 1)
                nc.gpsimd.tensor_tensor(tile_of(v_pair, at.n, DIM, 2 * DIM), v_f32[at.u][:, :],
                                        tile_of(v_pair, at.n, 0, DIM), ALU.subtract
                                        ).then_inc(v_lo_ready, 1)

            with pool.Fori(0, TILES // 2) as i:
                low_v(At(i, 0))
                low_v(At(i, 1))

        @block.tensor
        def _(pe):
            pe.wait_ge(ident_ready, 1)
            pe.wait_ge(wv_loaded, 16)
            for k in range(KC):
                for e in range(KC):
                    mm = pe.transpose(wvT_bank[k][:, e, :], wv_sb[:, e, k * P:(k + 1) * P], ident[:, :])
                mm.then_inc(wvT_ready, 1)
            pe.wait_ge(wqk_loaded, 32)
            pe.wait_ge(wide_ready, 2 * KC)
            for dst, lhs, rhs in ((u_bank, b_wide, wk_sb), (w_bank, bk_wide, wq_sb)):
                for e in range(KC):
                    pe.matmul(dst, lhs[:, e, :], rhs[:, e, :], start=(e == 0), stop=(e == KC - 1))
            for e in range(KC):
                mm = pe.matmul(bq_bk_bank, bk_wide[:, e, :], b_cols[:, 0, e:e + 1],
                               start=(e == 0), stop=(e == KC - 1))
            mm.then_inc(bias_products_ready, 1)

            def product_m(d):
                if d == 1:
                    pe.wait_ge(wvT_scaled_lo, KC)
                if d == KC - 1:
                    pe.wait_ge(u_copied, 1)
                for e in range(KC):
                    mm = pe.matmul(m_bank[d], wq_sb[:, e, d * P:(d + 1) * P], wk_sb[:, e, :],
                                   start=(e == 0), stop=(e == KC - 1))
                mm.then_inc(m_ready, 1)

            def transpose_h(at):
                pe.wait_ge(normed, at.n + 1)
                if due(at.n - 1):
                    pe.wait_ge(hT_lo_ready, at.n - 1)
                for k in range(KC):
                    mm = pe.transpose(hT_bank[at.u][:, k, :], normal[at.u][:, k * P:(k + 1) * P],
                                      ident[:, :])
                mm.then_inc(hT_ready, 1)

            def project_v(at):
                pe.wait_ge(hT_lo_ready, at.n + 1)
                if due(at.n - 1):
                    pe.wait_ge(v_copied, at.n - 1)
                for k in range(KC):
                    for j, (a, b) in enumerate(((hT_hi, wvT_hi), (hT_hi, wvT_lo), (hT_lo, wvT_hi))):
                        mm = pe.matmul(v_bank[at.u][:, :], cols(a, k, at.n), b[:, k, :],
                                       start=(k == 0 and j == 0), stop=(k == KC - 1 and j == 2))
                mm.then_inc(v_ready, 1)

            def fold_t(at):
                if due(at.n):
                    pe.wait_ge(t_copied, at.n)
                for k in range(KC):
                    for j, (a, b) in enumerate(((hT_hi, m_hi), (hT_hi, m_lo), (hT_lo, m_hi))):
                        mm = pe.matmul(t_bank[:, :], cols(a, k, at.n), b[:, k, :],
                                       start=(k == 0 and j == 0), stop=(k == KC - 1 and j == 2))
                mm.then_inc(t_ready, 1)

            def transpose_t(at):
                pe.wait_ge(t_copied, at.n + 1)
                if due(at.n):
                    pe.wait_ge(tT_lo_ready, at.n)
                for k in range(KC):
                    mm = pe.transpose(tT_bank[:, k, :], t_rows[:, k * P:(k + 1) * P], ident[:, :])
                mm.then_inc(tT_ready, 1)

            def scores(at, c):
                if c == 0:
                    pe.wait_ge(tT_lo_ready, at.n + 1)
                if due(CHUNKS * at.n + c - 1):
                    pe.wait_ge(scored, CHUNKS * at.n + c - 1)
                if known(at.n) and at.n == 0 and c < 2:
                    pe.wait_ge(v_copied, TILES - 1 + c)
                span = slice(c * CHUNK, (c + 1) * CHUNK)
                for k in range(KC):
                    for j, (a, b) in enumerate(((tT_hi, hT_hi), (tT_hi, hT_lo), (tT_lo, hT_hi))):
                        mm = pe.matmul(z_bank[c % 2][:, :], a[at.u][:, k, :], b[:, k, span],
                                       start=(k == 0 and j == 0), stop=(k == KC - 1 and j == 2))
                mm.then_inc(z_ready, 1)

            def weigh_v(at, c):
                if c == 0 and known(at.n) and at.n == 0:
                    pe.wait_ge(v_lo_ready, TILES)
                if c == 0:
                    if due(at.n - 1):
                        pe.wait_ge(o_scaled, at.n - 1)
                pe.wait_ge(moved_by_vector, CHUNKS * at.n + c + 1)
                pe.wait_ge(moved_by_scalar, CHUNKS * at.n + c + 1)
                for b in range(BLOCKS):
                    j = c * BLOCKS + b
                    for s, (part, off) in enumerate(((0, 0), (0, DIM), (1, 0))):
                        mm = pe.matmul(o_bank[at.u][:, :], pT_pair[c % 2][:, b, :, part],
                                       v_pair[:, j, off:off + DIM],
                                       start=(c == 0 and b == 0 and s == 0),
                                       stop=(c == CHUNKS - 1 and b == BLOCKS - 1 and s == 2))
                mm.then_inc(pv_done, 1)

            def step(at, own=True, prev=True, older=True, fold=True):
                for c in range(CHUNKS):
                    if own:
                        scores(at, c)
                    if c == 0 and older:
                        weigh_v(at.back(2), CHUNKS - 1)
                    if c > 0 and prev:
                        weigh_v(at.back(), c - 1)
                    if c == 2 and fold:
                        fold_t(at.back(-1))
                    if c == 3 and fold:
                        transpose_t(at.back(-1))

            def group(g, fold=False):
                for j in range(GROUP):
                    at = tile_in(g, j)
                    if not (known(at.n) and at.n <= 1):
                        transpose_h(at)
                    if not (known(at.n) and at.n == 0):
                        project_v(at.back())
                    if fold and j == 0:
                        fold_t(At(0, 0))
                    if fold and j == 1:
                        transpose_t(At(0, 0))

            product_m(0)
            product_m(1)
            transpose_h(At(0, 0))
            product_m(2)
            transpose_h(At(0, 1))
            product_m(3)
            pe.wait_ge(bqbk_copied, 1)
            group(0)
            with pe.Fori(1, GROUPS - 1) as g:
                group(g)
            pe.wait_ge(m_scaled_lo, KC)
            group(GROUPS - 1, fold=True)
            project_v(tile_in(GROUPS - 1, GROUP - 1))
            step(At(0, 0), prev=False, older=False)
            step(At(0, 1), older=False)
            with pe.Fori(1, TILES // 2 - 1) as i:
                step(At(i, 0))
                step(At(i, 1))
            last = TILES // 2 - 1
            step(At(last, 0))
            step(At(last, 1), fold=False)
            step(At(last + 1, 0), own=False, fold=False)
            weigh_v(At(last, 1), CHUNKS - 1)

        @block.scalar
        def _(act):
            def flat(ap3):
                return ap3.rearrange("p k n -> p (k n)")

            act.wait_ge(scales_ready, 1)
            for k in range(KC):
                act.wait_ge(wvT_ready, k + 1)
                nc.scalar.activation(wvT_hi[:, k, :], flat(wvT_bank[k]), ACT.Copy, scale=up[0][:, 0:1]
                                     ).then_inc(wvT_scaled_hi, 1)

            def square_root(g):
                act.wait_ge(var_ready, g + 1)
                span = slice(g * GROUP, (g + 1) * GROUP) if known(g) else bass.ds(g * GROUP, GROUP)
                nc.scalar.activation(root[:, span], var_eps[:, span], ACT.Sqrt).then_inc(root_ready, 1)

            square_root(0)
            square_root(1)

            def high_h(at):
                act.wait_ge(hT_ready, at.n + 1)
                nc.scalar.activation(wide(hT_hi, at.n), hT_bank[at.u][:, :, :], ACT.Relu
                                     ).then_inc(hT_hi_ready, 1)

            def copy_v(at):
                act.wait_ge(v_ready, at.n + 1)
                nc.scalar.copy(tile_of(v_pair, at.n, 0, DIM), v_bank[at.u][:, :])
                if due(at.n - 1):
                    act.wait_ge(v_lo_ready, at.n - 1)
                nc.scalar.copy(v_f32[at.u][:, :], v_bank[at.u][:, :]).then_inc(v_copied, 1)

            def high_m(k):
                act.wait_ge(scales_ready, 2)
                nc.scalar.activation(m_hi[:, k, :], m_f32[:, k, :], ACT.Copy, scale=up[1][:, 0:1]
                                     ).then_inc(m_scaled_hi, 1)

            def copy_m(d):
                act.wait_ge(m_ready, d + 1)
                nc.scalar.copy(m_f32[:, d, :], m_bank[d]).then_inc(m_copied, 1)

            def group(g, roots=True, own_m=False, own_t=False):
                for j in range(GROUP):
                    at = tile_in(g, j)
                    if not (known(at.n) and at.n <= 1):
                        high_h(at)
                    if not (known(at.n) and at.n == 0):
                        copy_v(at.back())
                    if own_m and j >= 2:
                        high_m(2 * j - 4)
                        high_m(2 * j - 3)
                    if j == 0 and roots:
                        square_root(g + 1)
                    if own_t and j == 2:
                        high_t(At(0, 0))

            def high_t(at):
                act.wait_ge(tT_ready, at.n + 1)
                nc.scalar.copy(tT_hi[at.u][:, :, :], tT_bank[:, :, :]).then_inc(tT_hi_ready, 1)

            def exp(at, c):
                if c == 0:
                    act.wait_ge(max_ready, at.n + 1)
                if due(CHUNKS * at.n + c - 1):
                    act.wait_ge(p_lo_ready, CHUNKS * at.n + c - 1)
                nc.scalar.activation(p_bank[c % 2][:, :], ring[at.u][:, c * CHUNK:(c + 1) * CHUNK], ACT.Exp,
                                     bias=neg_max[at.u][:, 0:1], scale=gain[:, 0:1],
                                     accum_out=sums[at.u][:, c:c + 1]).then_inc(p_ready, 1)

            def high_p(at, c):
                act.wait_ge(p_ready, CHUNKS * at.n + c + 1)
                if due(CHUNKS * at.n + c - 1):
                    act.wait_ge(turned, CHUNKS * at.n + c - 1)
                nc.scalar.mul(p_pair[c % 2][:, :, 0], p_bank[c % 2][:, :], P_SCALE
                              ).then_inc(p_hi_ready, 1)

            def move_p(at, c, share):
                act.wait_ge(turned, CHUNKS * at.n + c + 1)
                if due(CHUNKS * at.n + c - 1):
                    act.wait_ge(pv_done, CHUNKS * at.n + c - 1)
                quadrant_moves(nc.scalar.copy, c % 2, share).then_inc(moved_by_scalar, 1)

            def step(at, prev=True, fold=True, share=(0, 1)):
                for c in range(CHUNKS):
                    if prev:
                        exp(at.back(), c)
                        high_p(at.back(), c)
                        if c:
                            move_p(at.back(), c - 1, share)
                    if c == 5 and fold:
                        high_t(at.back(-1))
                if prev:
                    move_p(at.back(), CHUNKS - 1, share)

            copy_m(0)
            copy_m(1)
            high_h(At(0, 0))
            copy_m(2)
            high_h(At(0, 1))
            copy_m(3)
            group(0, roots=False, own_m=True)
            with act.Fori(1, GROUPS - 1) as g:
                group(g)
            group(GROUPS - 1, roots=False, own_t=True)
            copy_v(tile_in(GROUPS - 1, GROUP - 1))
            step(At(0, 0), prev=False)
            step(At(0, 1))
            with act.Fori(1, TILES // 2 - 1) as i:
                step(At(i, 0))
                step(At(i, 1))
            last = TILES // 2 - 1
            step(At(last, 0))
            step(At(last, 1), fold=False)
            step(At(last + 1, 0), fold=False, share=(0,))

        @block.vector
        def _(dve):
            v = nc.vector
            seq = [0]

            def link(ins):
                seq[0] += 1
                ins.then_inc(scale_seq, 1)
                dve.wait_ge(scale_seq, seq[0])

            def flat(ap3):
                return ap3.rearrange("p k n -> p (k n)")

            def magnitude(k):
                dve.wait_ge(mag_reduced, k + 1)
                link(v.tensor_reduce(top[k][:, :], mag_all[k][:, :], AX_X, ALU.max))
                link(v.tensor_scalar(top[k][:, :], top[k][:, :], TINY, None, ALU.max))
                link(v.tensor_scalar(up_inv[k][:, :].bitcast(I32), top[k][:, :].bitcast(I32), EXPONENT, None,
                                     ALU.bitwise_and))
                link(v.tensor_scalar(up_inv[k][:, :], up_inv[k][:, :], 1.0 / HEADROOM, None, ALU.mult))
                v.reciprocal(up[k][:, :], up_inv[k][:, :]).then_inc(scales_ready, 1)
                dve.wait_ge(scales_ready, k + 1)

            def row_stats(n, j):
                v.bn_stats(stats[:, j, :], tile_of(rows, n, 0, DIM)).then_inc(stats_ready, 1)

            def aggregate(j):
                v.bn_aggr(mean_var[:, j, :], stats[:, j, :]).then_inc(aggregated, 1)

            def group_span(g):
                return slice(g * GROUP, (g + 1) * GROUP) if known(g) else bass.ds(g * GROUP, GROUP)

            def group_var(g):
                dve.wait_ge(aggregated, GROUP * g + GROUP)
                v.tensor_copy(mean[:, group_span(g)], mean_var[:, :, 0])
                v.tensor_scalar(var_eps[:, group_span(g)], mean_var[:, :, 1], EPS, None, ALU.add
                                ).then_inc(var_ready, 1)

            def group_rstd(g):
                r, span = rstd[:, group_span(g)], group_span(g)
                dve.wait_ge(root_ready, g + 1)
                v.reciprocal(r, root[:, span]).then_inc(inv_root, 1)
                dve.wait_ge(inv_root, g + 1)
                v.tensor_tensor(newton[:, :], r, r, ALU.mult).then_inc(newton_seq, 1)
                dve.wait_ge(newton_seq, 2 * g + 1)
                v.scalar_tensor_tensor(out=newton[:, :], in0=newton[:, :], scalar=-0.5, in1=var_eps[:, span],
                                       op0=ALU.mult, op1=ALU.mult).then_inc(newton_seq, 1)
                dve.wait_ge(newton_seq, 2 * g + 2)
                v.scalar_tensor_tensor(out=r, in0=newton[:, :], scalar=1.5, in1=r,
                                       op0=ALU.add, op1=ALU.mult).then_inc(rstd_ready, 1)

            def normalise(at):
                n = slice(at.n, at.n + 1) if known(at.n) else bass.ds(at.n, 1)
                if due(at.n - 1):
                    dve.wait_ge(hT_ready, at.n - 1)
                if due(at.n - 1):
                    dve.wait_ge(dots_done, at.n - 1)
                v.tensor_scalar(normal[at.u][:, :], tile_of(rows, at.n, 0, DIM), mean[:, n], rstd[:, n],
                                ALU.subtract, ALU.mult).then_inc(normed, 1)

            def largest(dst, src):
                return v.tensor_reduce(dst, src, AX_X, ALU.max, apply_absolute_value=True)

            dve.wait_ge(zeros_ready, 1)
            dve.wait_ge(bias_loaded, 32)
            for j, w in enumerate((b_wide, bk_wide)):
                for k in range(KC):
                    v.tensor_scalar(w[:, k, :], zeros[:, :], b_cols[:, j, k:k + 1], None, ALU.add
                                    ).then_inc(wide_ready, 1)
            dve.wait_ge(wv_loaded, 16)
            for k in range(KC):
                last = largest(mag_v[:, k:k + 1], wv_sb[:, k, :])
            last.then_inc(mag_ready, 1)
            magnitude(0)
            v.tensor_scalar(out_gain[:, :], up_inv[0][:, :], 1.0 / P_SCALE, None, ALU.mult)
            for k in range(KC):
                dve.wait_ge(wvT_scaled_hi, k + 1)
                v.scalar_tensor_tensor(out=wvT_lo[:, k, :], in0=flat(wvT_bank[k]), scalar=up[0][:, 0:1],
                                       in1=wvT_hi[:, k, :], op0=ALU.mult, op1=ALU.subtract
                                       ).then_inc(wvT_scaled_lo, 1)
            for g in range(2):
                dve.wait_ge(x_loaded, 16 * g + 16)
                for j in range(GROUP):
                    row_stats(GROUP * g + j, j)
                    dve.wait_ge(stats_ready, GROUP * g + j + 1)
                    aggregate(j)
                group_var(g)
            group_rstd(0)
            group_rstd(1)
            dve.wait_ge(bias_products_ready, 1)
            dve.wait_ge(rstd_ready, 2)
            normalise(At(0, 0))
            normalise(At(0, 1))
            v.tensor_copy(w_all[:, :], w_bank).then_inc(w_copied, 1)
            v.tensor_copy(bq_bk[:, :], bq_bk_bank).then_inc(bqbk_copied, 1)
            v.tensor_copy(u_all[:, :], u_bank).then_inc(u_copied, 1)
            def row_dot(at):
                dve.wait_ge(normed, at.n + 1)
                if due(at.n):
                    dve.wait_ge(dots_done, at.n)
                at_n = slice(at.n, at.n + 1) if known(at.n) else bass.ds(at.n, 1)
                v.scalar_tensor_tensor(out=dot_waste[:, :], in0=normal[at.u][:, :], scalar=0.0,
                                       in1=w_all[:, :], op0=ALU.max, op1=ALU.mult,
                                       accum_out=s_all[:, at_n]).then_inc(dots_done, 1)

            def low_h(at):
                dve.wait_ge(hT_hi_ready, at.n + 1)
                v.scalar_tensor_tensor(out=wide(hT_lo, at.n), in0=hT_bank[at.u][:, :, :], scalar=0.0,
                                       in1=wide(hT_hi, at.n), op0=ALU.max, op1=ALU.subtract
                                       ).then_inc(hT_lo_ready, 1)

            def largest_m(k):
                dve.wait_ge(m_copied, k + 1)
                return largest(mag_m[:, k:k + 1], m_f32[:, k, :])

            def scale_m():
                v.tensor_scalar(mag_m[:, KC:KC + 1], mag_m[:, KC:KC + 1], 1.0 / DIM, None, ALU.mult
                                ).then_inc(mag_ready, 1)
                magnitude(1)
                link(v.tensor_scalar(gain[:, :], up_inv[1][:, :], SCALE, None, ALU.mult))
                v.tensor_scalar(neg_gain[:, :], gain[:, :], -1.0, None, ALU.mult)
                link(v.reciprocal(gain_inv[:, :], gain[:, :]))
                v.tensor_scalar(masked_at[:, :], gain_inv[:, :], MASKED, None, ALU.mult)
                v.tensor_scalar(u_all[:, :], u_all[:, :], up[1][:, 0:1], None, ALU.mult
                                ).then_inc(u_scaled, 1)

            def low_m(k):
                dve.wait_ge(m_scaled_hi, k + 1)
                v.scalar_tensor_tensor(out=m_lo[:, k, :], in0=m_f32[:, k, :], scalar=up[1][:, 0:1],
                                       in1=m_hi[:, k, :], op0=ALU.mult, op1=ALU.subtract
                                       ).then_inc(m_scaled_lo, 1)

            def group(g, stats_too=True, roots=True, own_m=False, own_t=False, more=True):
                for j in range(GROUP):
                    at = tile_in(g, j)
                    if stats_too:
                        if j == 0:
                            dve.wait_ge(x_loaded, 16 * g + 48)
                        row_stats(at.n + 2 * GROUP, j)
                    if not (known(at.n) and at.n <= 1):
                        low_h(at)
                    if (j < GROUP - 1 or more) and not (known(at.n) and at.n == 0):
                        if j == GROUP - 1:
                            dve.wait_ge(rstd_ready, g + 2)
                        if stats_too:
                            dve.wait_ge(stats_ready, at.n + 2 * GROUP + 1)
                        normalise(at.back(-1))
                    elif stats_too:
                        dve.wait_ge(stats_ready, at.n + 2 * GROUP + 1)
                    if stats_too:
                        aggregate(j)
                    row_dot(at)
                    if j == 1 and roots:
                        group_rstd(g + 1)
                    if own_m and j == 1:
                        scale_m()
                    if own_m and j >= 2:
                        low_m(2 * j - 4)
                        low_m(2 * j - 3)
                    if own_t and j == 1:
                        copy_t(At(0, 0))
                    if own_t and j == 2:
                        low_t(At(0, 0))
                if stats_too:
                    group_var(g + 2)

            def copy_t(at):
                dve.wait_ge(t_ready, at.n + 1)
                if due(at.n):
                    dve.wait_ge(tT_ready, at.n)
                v.tensor_tensor(t_rows[:, :], t_bank[:, :], u_all[:, :], ALU.add).then_inc(t_copied, 1)

            def copy_s(at):
                col = s_all[:, at.n:at.n + 1] if known(at.n) else s_all[:, bass.ds(at.n, 1)]
                v.tensor_copy(s_tile[at.u][:, :], col).then_inc(s_tile_ready, 1)

            def low_t(at):
                dve.wait_ge(tT_hi_ready, at.n + 1)
                v.tensor_tensor(tT_lo[at.u][:, :, :], tT_bank[:, :, :], tT_hi[at.u][:, :, :], ALU.subtract
                                ).then_inc(tT_lo_ready, 1)

            def mask(at, c):
                g = CHUNKS * at.n + c
                part = ring[at.u][:, c * CHUNK:(c + 1) * CHUNK]
                dve.wait_ge(z_ready, g + 1)
                if c == 0:
                    dve.wait_ge(s_tile_ready, at.n + 1)
                if c % 2 == 0:
                    dve.wait_ge(adj_loaded[at.u][c // 2], 16 * at.half + 16)
                v.scalar_tensor_tensor(out=part, in0=z_bank[c % 2][:, :], scalar=s_tile[at.u][:, 0:1], in1=part,
                                       op0=ALU.add, op1=ALU.mult).then_inc(scored, 1)
                dve.wait_ge(scored, g + 1)
                v.tensor_scalar(penalty[c % 2][:, :], part, 0.0, masked_at[:, 0:1], ALU.is_equal, ALU.mult
                                ).then_inc(penalised, 1)
                dve.wait_ge(scales_ready, 2)
                dve.wait_ge(penalised, g + 1)
                start = LOWEST if c == 0 else run_max[at.u][:, c - 1:c]
                if c:
                    dve.wait_ge(masked, g)
                v.tensor_tensor_reduce(out=part, in0=part, in1=penalty[c % 2][:, :], scale=1.0, scalar=start,
                                       op0=ALU.add, op1=ALU.max, accum_out=run_max[at.u][:, c:c + 1]
                                       ).then_inc(masked, 1)

            def finish_max(at):
                dve.wait_ge(masked, CHUNKS * at.n + CHUNKS)
                v.tensor_scalar(neg_max[at.u][:, :], run_max[at.u][:, CHUNKS - 1:CHUNKS], neg_gain[:, 0:1], None,
                                ALU.mult).then_inc(max_ready, 1)

            def low_p(at, c):
                dve.wait_ge(p_hi_ready, CHUNKS * at.n + c + 1)
                v.scalar_tensor_tensor(out=p_pair[c % 2][:, :, 1], in0=p_bank[c % 2][:, :], scalar=P_SCALE,
                                       in1=p_pair[c % 2][:, :, 0], op0=ALU.mult, op1=ALU.subtract
                                       ).then_inc(p_lo_ready, 1)

            def turn_p(at, c, share):
                g = CHUNKS * at.n + c
                dve.wait_ge(p_lo_ready, g + 1)
                if due(g - 1):
                    dve.wait_ge(moved_by_scalar, g - 1)
                if due(g - 1):
                    dve.wait_ge(moved_by_vector, g - 1)
                v.transpose(p_turned[c % 2][:, :, :].rearrange("p c s -> p (c s)").bitcast(U32),
                            p_pair[c % 2][:, :, :].rearrange("p c s -> p (c s)").bitcast(U32)
                            ).then_inc(turned, 1)
                dve.wait_ge(turned, g + 1)
                if due(g - 1):
                    dve.wait_ge(pv_done, g - 1)
                quadrant_moves(v.tensor_copy, c % 2, share).then_inc(moved_by_vector, 1)

            def row_gain(at):
                dve.wait_ge(p_ready, CHUNKS * at.n + CHUNKS)
                v.tensor_reduce(row_sum[:, :], sums[at.u][:, :], AX_X, ALU.add).then_inc(sum_ready, 1)
                dve.wait_ge(sum_ready, at.n + 1)
                v.reciprocal(row_inv[:, :], row_sum[:, :]).then_inc(inv_ready, 1)
                dve.wait_ge(inv_ready, at.n + 1)
                v.tensor_tensor(row_out[at.u][:, :], row_inv[:, :], out_gain[:, :], ALU.mult
                                ).then_inc(row_out_ready, 1)

            def finish(at):
                if due(16 * at.n):
                    dve.wait_ge(stored, 16 * at.n)
                dve.wait_ge(row_out_ready, at.n + 1)
                dve.wait_ge(pv_done, CHUNKS * at.n + CHUNKS)
                v.scalar_tensor_tensor(out=o_rows[:, :], in0=o_bank[at.u][:, :],
                                       scalar=row_out[at.u][:, 0:1], in1=bv_all[:, :],
                                       op0=ALU.mult, op1=ALU.add).then_inc(o_scaled, 1)
                dve.wait_ge(x_back, 16 * at.n + 16)
                dve.wait_ge(o_scaled, at.n + 1)
                v.scalar_tensor_tensor(out=o_rows[:, :], in0=o_rows[:, :], scalar=0.0,
                                       in1=x_again[:, :], op0=ALU.max, op1=ALU.add
                                       ).then_inc(finished, 1)

            def step(at, own=True, prev=True, fold=True, older=True, share=(2, 3)):
                for c in range(CHUNKS):
                    if c == 3 and fold:
                        copy_t(at.back(-1))
                        copy_s(at.back(-1))
                    if prev:
                        low_p(at.back(), c)
                        turn_p(at.back(), c, share)
                    if own:
                        mask(at, c)
                        if c == CHUNKS - 1:
                            finish_max(at)
                    if c == 1 and older:
                        finish(at.back(2))
                    if c == 5 and fold:
                        low_t(at.back(-1))
                if prev:
                    row_gain(at.back())

            dve.wait_ge(w_copied, 1)
            dve.wait_ge(u_copied, 1)
            largest(mag_m[:, KC:KC + 1], u_all[:, :])
            largest_m(0)
            largest_m(1)
            low_h(At(0, 0))
            largest_m(2)
            low_h(At(0, 1))
            link(largest_m(3))
            group(0, roots=False, own_m=True)
            with dve.Fori(1, GROUPS - 2) as g:
                group(g)
            group(GROUPS - 2, stats_too=False)
            group(GROUPS - 1, stats_too=False, roots=False, own_t=True, more=False)
            dve.wait_ge(dots_done, TILES)
            v.tensor_scalar(s_all[:, :], s_all[:, :], bq_bk[:, 0:1], up[1][:, 0:1], ALU.add, ALU.mult
                            ).then_inc(s_all_ready, 1)
            dve.wait_ge(s_all_ready, 1)
            copy_s(At(0, 0))
            dve.wait_ge(bv_loaded, 16)
            dve.wait_ge(v_lo_ready, TILES)
            step(At(0, 0), prev=False, older=False)
            step(At(0, 1), older=False)
            step(At(1, 0))
            step(At(1, 1))
            with dve.Fori(2, TILES // 2 - 1) as i:
                step(At(i, 0))
                step(At(i, 1))
            last = TILES // 2 - 1
            step(At(last, 0))
            step(At(last, 1), fold=False)
            step(At(last + 1, 0), own=False, fold=False, share=(1, 2, 3))
            finish(At(last, 1))


_INS = ["x", "adj", "L0_gnn_W_q", "L0_gnn_b_q", "L0_gnn_W_k", "L0_gnn_b_k", "L0_gnn_W_v", "L0_gnn_b_v"]


def kernel(**inputs):
    import numpy as _np
    import concourse.bacc as _bacc
    from concourse import mybir as _mybir
    from concourse.bass_utils import run_bass_kernel_spmd as _run

    nc = _bacc.Bacc("TRN2", target_bir_lowering=False, num_devices=1)
    arrays, args = {}, []
    for name in _INS:
        a = _np.ascontiguousarray(inputs[name])
        arrays[f"in_{name}"] = a
        args.append(nc.dram_tensor(f"in_{name}", a.shape, _mybir.dt.from_np(a.dtype), kind="ExternalInput").ap())
    out = nc.dram_tensor("out", (NODES, DIM), F32, kind="ExternalOutput").ap()
    adj_preln_attention(nc, *args, out)
    r = _run(nc, [arrays], core_ids=[0])
    return r.results[0]["out"]
```

```python
from contextlib import ExitStack

import concourse.bass as bass
from concourse import mybir

F32 = mybir.dt.float32
F16 = mybir.dt.float16
I32 = mybir.dt.int32
U32 = mybir.dt.uint32
ALU = mybir.AluOpType
ACT = mybir.ActivationFunctionType
AX_X = mybir.AxisListType.X
ABSMAX = bass.bass_isa.ReduceOp.absmax

P = 128
NODES = 4096
DIM = 512
KC = DIM // P
TILES = NODES // P
PAIR = 2
CHUNK = 512
CHUNKS = NODES // CHUNK
BLOCKS = CHUNK // P
BATCH = 2
BATCHES = CHUNKS // BATCH
SQ = 32
QUADS = P // SQ
QUARTERS = 4
GROUP = 4
GROUPS = TILES // GROUP
EPS = 1e-5
SCALE = 1.0 / DIM ** 0.5
MASKED = -10000.0
LOWEST = -3.0e38
TINY = 1e-30
EXPONENT = 0x7F800000
WARM_UPS = 9
HEADROOM = 16.0
P_SCALE = 16384.0


def adj_preln_attention(nc, x, adj, wq, bq, wk, bk, wv, bv, out):
    ctx = ExitStack()
    with ctx:
        def sb(name, shape, dt):
            return ctx.enter_context(nc.sbuf_tensor(name, shape, dt))

        def pb(name, shape, dt=F32):
            return ctx.enter_context(nc.psum_tensor(name, shape, dt))

        def sem(name):
            return ctx.enter_context(nc.semaphore(name))

        hT_hi = sb("hT_hi", [P, KC, NODES], F16)
        hT_lo = sb("hT_lo", [P, KC, NODES], F16)
        rows = sb("rows", [P, TILES, DIM], F32)
        v_pair = rows[:, :, :].bitcast(F16)
        ring = [sb(f"ring{u}", [P, NODES], F32) for u in range(2)]
        m_hi = sb("m_hi", [P, KC, DIM], F16)
        m_lo = sb("m_lo", [P, KC, DIM], F16)
        p_pair = [sb(f"p_pair{u}", [P, CHUNK, 2], F16) for u in range(2)]
        p_turned = [sb(f"p_turned{u}", [P, BATCH * CHUNK, 2], F16) for u in range(2)]
        pT_pair = [sb(f"pT_pair{u}", [P, BATCH * BLOCKS, P, 2], F16) for u in range(2)]
        penalty = [sb(f"penalty{u}", [P, CHUNK], F32) for u in range(2)]
        tT_hi = [sb(f"tT_hi{u}", [P, KC, P], F16) for u in range(2)]
        tT_lo = [sb(f"tT_lo{u}", [P, KC, P], F16) for u in range(2)]
        tT_f32 = sb("tT_f32", [P, KC, P], F32)
        u_cols = sb("u_cols", [P, KC], F32)
        x_again = sb("x_again", [P, DIM], F32)
        o_rows = sb("o_rows", [P, DIM], F32)
        ident = sb("ident", [P, P], F32)
        s_all = sb("s_all", [P, TILES], F32)
        s_tile = [sb(f"s_tile{u}", [P, 1], F32) for u in range(2)]
        run_max = [sb(f"run_max{u}", [P, CHUNKS], F32) for u in range(2)]
        neg_max = [sb(f"neg_max{u}", [P, 1], F32) for u in range(2)]
        sums = [sb(f"sums{u}", [P, CHUNKS], F32) for u in range(2)]
        bv_all = sb("bv_all", [P, DIM], F32)
        row_sum = sb("row_sum", [P, 1], F32)
        row_inv = sb("row_inv", [P, 1], F32)
        row_out = [sb(f"row_out{u}", [P, 1], F32) for u in range(2)]
        mag_v = sb("mag_v", [P, KC], F32)
        mag_m = sb("mag_m", [P, KC + 1], F32)
        mag = [mag_v, mag_m]
        mag_all = [sb("mag_all_v", [P, KC], F32), sb("mag_all_m", [P, KC + 1], F32)]
        top = [sb(f"top{k}", [P, 1], F32) for k in range(2)]
        up = [sb(f"up{k}", [P, 1], F32) for k in range(2)]
        up_inv = [sb(f"up_inv{k}", [P, 1], F32) for k in range(2)]
        gain = sb("gain", [P, 1], F32)
        neg_gain = sb("neg_gain", [P, 1], F32)
        gain_inv = sb("gain_inv", [P, 1], F32)
        masked_at = sb("masked_at", [P, 1], F32)
        out_gain = sb("out_gain", [P, 1], F32)
        bq_bk = sb("bq_bk", [P, 1], F32)
        b_cols = sb("b_cols", [P, 2, KC], F32)
        zeros = sb("zeros", [P, P], F32)
        stats = sb("stats", [P, GROUP, 6], F32)
        mean_var = sb("mean_var", [P, GROUP, 2], F32)
        mean = sb("mean", [P, TILES], F32)
        var_eps = sb("var_eps", [P, TILES], F32)
        root = sb("root", [P, TILES], F32)
        rstd = sb("rstd", [P, TILES], F32)
        newton = sb("newton", [P, GROUP], F32)

        half = KC * DIM
        wv_sb = ring[0][:, 0:half].rearrange("p (k n) -> p k n", k=KC)
        wk_sb = ring[0][:, half:2 * half].rearrange("p (k n) -> p k n", k=KC)
        wq_sb = ring[1][:, 0:half].rearrange("p (k n) -> p k n", k=KC)
        wvT = ring[1][:, half:2 * half].bitcast(F16).rearrange("p (s k n) -> p s k n", s=2, k=KC)
        wvT_hi, wvT_lo = wvT[:, 0], wvT[:, 1]
        w_all = penalty[0]
        dot_waste = penalty[1]

        def as_rows(pair):
            return pair.rearrange("p c s -> p (c s)").bitcast(F32)

        v_f32 = [as_rows(b[:, :, :]) for b in p_pair]
        normal = [as_rows(p_turned[0][:, u * CHUNK:(u + 1) * CHUNK, :]) for u in range(2)]
        m_f32 = [as_rows(pT_pair[d // 2][:, :, :, :].rearrange("p m c s -> p (m c) s")
                         [:, d % 2 * CHUNK:(d % 2 + 1) * CHUNK, :]) for d in range(KC)]
        bk_wide = normal[0].rearrange("p (k n) -> p k n", k=KC)

        z_bank = [pb(f"z{u}", [P, CHUNK]) for u in range(2)]
        p_bank = [pb(f"p{u}", [P, CHUNK]) for u in range(2)]
        o_bank = [pb(f"o{u}", [P, DIM]) for u in range(2)]
        tT_banks = pb("tT", [P, KC, PAIR * P])
        tT_bank = [tT_banks[:, b * KC // 2:(b + 1) * KC // 2, :].rearrange("p k n -> p (k n)") for b in range(2)]
        hT_bank = [b[:, :].rearrange("p (k n) -> p k n", k=KC) for b in p_bank]
        wvT_bank = hT_bank + [b.rearrange("p (k n) -> p k n", k=KC) for b in tT_bank]
        u_bank, w_bank, bq_bk_bank = o_bank[0][:, 0:KC], o_bank[1][:, :], z_bank[0][:, 0:1]
        m_bank = [z_bank[1][:, :], tT_bank[0], tT_bank[1], o_bank[1][:, :]]
        v_bank = z_bank

        wv_loaded = sem("wv_loaded")
        wq_loaded = sem("wq_loaded")
        wk_loaded = sem("wk_loaded")
        bias_loaded = sem("bias_loaded")
        bv_loaded = sem("bv_loaded")
        x_loaded = sem("x_loaded")
        x_back = sem("x_back")
        stored = sem("stored")
        ident_zero = sem("ident_zero")
        ident_ready = sem("ident_ready")
        zeros_ready = sem("zeros_ready")
        wvT_ready = sem("wvT_ready")
        wide_ready = sem("wide_ready")
        m_ready = sem("m_ready")
        bk_products_ready = sem("bk_products_ready")
        u_ready = sem("u_ready")
        m_copied = sem("m_copied")
        u_copied = sem("u_copied")
        w_copied = sem("w_copied")
        bqbk_copied = sem("bqbk_copied")
        mag_ready = sem("mag_ready")
        mag_reduced = sem("mag_reduced")
        scale_seq = sem("scale_seq")
        scales_ready = sem("scales_ready")
        wvT_scaled_hi = sem("wvT_scaled_hi")
        wvT_scaled_lo = sem("wvT_scaled_lo")
        m_scaled_hi = sem("m_scaled_hi")
        m_scaled_lo = sem("m_scaled_lo")
        u_scaled = sem("u_scaled")
        stats_ready = sem("stats_ready")
        aggregated = sem("aggregated")
        var_ready = sem("var_ready")
        root_ready = sem("root_ready")
        inv_root = sem("inv_root")
        newton_seq = sem("newton_seq")
        rstd_ready = sem("rstd_ready")
        normed = sem("normed")
        hT_ready = sem("hT_ready")
        hT_hi_ready = sem("hT_hi_ready")
        hT_lo_ready = sem("hT_lo_ready")
        dots_done = sem("dots_done")
        v_ready = sem("v_ready")
        v_copied = sem("v_copied")
        v_lo_ready = sem("v_lo_ready")
        s_all_ready = sem("s_all_ready")
        tT_ready = sem("tT_ready")
        tT_copied = sem("tT_copied")
        tT_hi_ready = sem("tT_hi_ready")
        tT_lo_ready = sem("tT_lo_ready")
        s_tile_ready = sem("s_tile_ready")
        z_ready = sem("z_ready")
        scored = sem("scored")
        penalised = sem("penalised")
        masked = sem("masked")
        max_ready = sem("max_ready")
        p_ready = sem("p_ready")
        p_hi_ready = sem("p_hi_ready")
        p_lo_ready = sem("p_lo_ready")
        turned = sem("turned")
        moved_by_vector = sem("moved_by_vector")
        moved_by_scalar = sem("moved_by_scalar")
        pv_done = sem("pv_done")
        sum_ready = sem("sum_ready")
        inv_ready = sem("inv_ready")
        row_out_ready = sem("row_out_ready")
        o_scaled = sem("o_scaled")
        finished = sem("finished")
        adj_loaded = [[sem(f"adj_loaded{u}{q}") for q in range(QUARTERS)] for u in range(2)]

        class At:

            def __init__(self, half, u):
                self.half, self.u, self.n = half, u, half * 2 + u

            def back(self, k=1):
                d = self.u - k
                return At(self.half + d // 2, d % 2)

        def known(v):
            return isinstance(v, int)

        def tile_in(g, j):
            return At(g * (GROUP // 2) + j // 2, j % 2)

        def due(count):
            return not known(count) or count > 0

        def wide(ap3, n):
            if known(n):
                return ap3[:, :, n * P:(n + 1) * P]
            return ap3[:, :, bass.ds(n * P, P)]

        def cols(ap3, k, n):
            if known(n):
                return ap3[:, k, n * P:(n + 1) * P]
            return ap3[:, k, bass.ds(n * P, P)]

        def tile_of(ap3, n, a, b):
            if known(n):
                return ap3[:, n, a:b]
            return ap3[:, bass.ds(n, 1), a:b].rearrange("p o d -> p (o d)")

        def quadrant_moves(copy, u, targets):
            for p in targets:
                for q in range(QUADS):
                    src = p_turned[u][q * SQ:(q + 1) * SQ, :, :].rearrange(
                        "c (m b a) s -> c m b (a s)", m=BATCH * BLOCKS, b=QUADS)[:, :, p, :]
                    dst = pT_pair[u][p * SQ:(p + 1) * SQ, :, q * SQ:(q + 1) * SQ, :].rearrange(
                        "c m a s -> c m (a s)")
                    ins = copy(dst, src)
            return ins

        block = ctx.enter_context(nc.Block())

        @block.sync
        def _(sp):
            sp.dma_start(wv_sb, wv.rearrange("(k p) n -> p k n", p=P)).then_inc(wv_loaded, 16)
            for j, b in enumerate((bq, bk)):
                sp.dma_start(b_cols[:, j, :], b.rearrange("(k p) -> p k", p=P),
                             allow_slow_non_contiguous=True).then_inc(bias_loaded, 16)
            sp.dma_start(wq_sb, wq.rearrange("(k p) n -> p k n", p=P)).then_inc(wq_loaded, 16)
            sp.dma_start(wk_sb, wk.rearrange("(k p) n -> p k n", p=P)).then_inc(wk_loaded, 16)

            x_groups = x.rearrange("(g t p) d -> g p t d", t=GROUP, p=P)
            sp.dma_start(rows[:, 0:GROUP, :], x_groups[0]).then_inc(x_loaded, 16)
            with sp.Fori(1, GROUPS) as g:
                first = sp.snap(g * GROUP)
                sp.wait_ge(x_loaded, 16 * g)
                sp.dma_start(rows[:, bass.ds(first, GROUP), :],
                             x_groups[bass.ds(g, 1)].rearrange("o p t d -> (o p) t d")
                             ).then_inc(x_loaded, 16)

            sp.dma_start(bv_all[:, :], bv.rearrange("(o n) -> o n", o=1).partition_broadcast(P)
                         .rearrange("p o n -> p (o n)")).then_inc(bv_loaded, 16)

            def start(n):
                return n * P if known(n) else sp.snap(n * P)

            def load_adj(at, row, q):
                w = NODES // QUARTERS
                sp.dma_start(ring[at.u][:, q * w:(q + 1) * w],
                             adj[bass.ds(row, P), q * w:(q + 1) * w]).then_inc(adj_loaded[at.u][q], 16)

            sp.wait_ge(u_ready, KC)
            for q in range(QUARTERS):
                load_adj(At(0, 0), 0, q)

            def step(at, has_next=True, stores=True, prev=True, reload=True):
                row, row_back, row_next = start(at.n - 2), start(at.n - 1), start(at.n + 1)
                for q in range(QUARTERS):
                    if has_next:
                        if prev:
                            sp.wait_ge(p_ready, CHUNKS * at.back().n + 2 * q + 2)
                        load_adj(at.back(-1), row_next, q)
                    if q == 1 and stores:
                        done = at.back(2)
                        sp.wait_ge(finished, done.n + 1)
                        sp.dma_start(out[bass.ds(row, P), :], o_rows[:, :]).then_inc(stored, 16)
                    if q == 2 and reload:
                        m = at.back()
                        if due(m.n):
                            sp.wait_ge(finished, m.n)
                        sp.dma_start(x_again[:, :], x[bass.ds(row_back, P), :]).then_inc(x_back, 16)

            sp.wait_ge(v_ready, TILES)
            step(At(0, 0), prev=False, stores=False, reload=False)
            step(At(0, 1), stores=False)
            step(At(1, 0))
            step(At(1, 1))
            with sp.Fori(2, TILES // 2 - 1) as i:
                step(At(i, 0))
                step(At(i, 1))
            last = TILES // 2 - 1
            step(At(last, 0))
            step(At(last, 1), has_next=False)
            step(At(last + 1, 0), has_next=False)
            step(At(last + 1, 1), has_next=False, reload=False)
            sp.wait_ge(stored, 16 * TILES)

        @block.gpsimd
        def _(pool):
            nc.gpsimd.memset(ident[:, :], 0.0).then_inc(ident_zero, 1)
            nc.gpsimd.memset(zeros[:, :], 0.0).then_inc(zeros_ready, 1)
            pool.wait_ge(ident_zero, 1)
            nc.gpsimd.affine_select(out=ident[:, :], in_=ident[:, :], compare_op=ALU.not_equal, fill=1.0,
                                    base=0, pattern=[[-1, P]], channel_multiplier=1
                                    ).then_inc(ident_ready, 1)
            pool.wait_ge(mag_ready, 1)
            nc.gpsimd.partition_all_reduce(mag_all[0][:, :], mag[0][:, :], P, ABSMAX).then_inc(mag_reduced, 1)

            def low_v(at):
                pool.wait_ge(v_copied, at.n + 1)
                nc.gpsimd.tensor_tensor(tile_of(v_pair, at.n, DIM, 2 * DIM), v_f32[at.u][:, :],
                                        tile_of(v_pair, at.n, 0, DIM), ALU.subtract
                                        ).then_inc(v_lo_ready, 1)

            split = (GROUPS - 2) * GROUP // 2
            with pool.Fori(0, split) as i:
                low_v(At(i, 0))
                low_v(At(i, 1))
            pool.wait_ge(mag_ready, 2)
            nc.gpsimd.partition_all_reduce(mag_all[1][:, :], mag[1][:, :], P, ABSMAX).then_inc(mag_reduced, 1)
            with pool.Fori(split, TILES // 2) as i:
                low_v(At(i, 0))
                low_v(At(i, 1))

        @block.tensor
        def _(pe):
            pe.wait_ge(ident_ready, 1)
            for _ in range(WARM_UPS):
                pe.matmul(m_bank[0][:, 0:P], ident[:, :], ident[:, :], start=True, stop=True)
            pe.wait_ge(wv_loaded, 16)
            for k in range(KC):
                for e in range(KC):
                    mm = pe.transpose(wvT_bank[k][:, e, :], wv_sb[:, e, k * P:(k + 1) * P], ident[:, :])
                mm.then_inc(wvT_ready, 1)
            pe.wait_ge(wide_ready, KC)
            pe.wait_ge(wq_loaded, 16)
            for e in range(KC):
                pe.matmul(w_bank, bk_wide[:, e, :], wq_sb[:, e, :], start=(e == 0), stop=(e == KC - 1))
            for e in range(KC):
                mm = pe.matmul(bq_bk_bank, bk_wide[:, e, :], b_cols[:, 0, e:e + 1],
                               start=(e == 0), stop=(e == KC - 1))
            mm.then_inc(bk_products_ready, 1)
            pe.wait_ge(wk_loaded, 16)

            def product_m(d):
                if d == 1:
                    pe.wait_ge(wvT_scaled_lo, KC)
                if d == KC - 1:
                    pe.wait_ge(w_copied, 1)
                for e in range(KC):
                    mm = pe.matmul(m_bank[d], wq_sb[:, e, d * P:(d + 1) * P], wk_sb[:, e, :],
                                   start=(e == 0), stop=(e == KC - 1))
                mm.then_inc(m_ready, 1)
                for e in range(KC):
                    mm = pe.matmul(u_bank[:, d:d + 1], wk_sb[:, e, d * P:(d + 1) * P], b_cols[:, 0, e:e + 1],
                                   start=(e == 0), stop=(e == KC - 1))
                mm.then_inc(u_ready, 1)

            def transpose_h(at):
                pe.wait_ge(normed, at.n + 1)
                if due(at.n - 1):
                    pe.wait_ge(hT_lo_ready, at.n - 1)
                for k in range(KC):
                    mm = pe.transpose(hT_bank[at.u][:, k, :], normal[at.u][:, k * P:(k + 1) * P],
                                      ident[:, :])
                mm.then_inc(hT_ready, 1)

            def project_v(at):
                pe.wait_ge(hT_lo_ready, at.n + 1)
                if due(at.n - 1):
                    pe.wait_ge(v_copied, at.n - 1)
                for k in range(KC):
                    for j, (a, b) in enumerate(((hT_hi, wvT_hi), (hT_hi, wvT_lo), (hT_lo, wvT_hi))):
                        mm = pe.matmul(v_bank[at.u][:, :], cols(a, k, at.n), b[:, k, :],
                                       start=(k == 0 and j == 0), stop=(k == KC - 1 and j == 2))
                mm.then_inc(v_ready, 1)

            def fold_t(pair, b):
                if b == 0 and known(pair) and pair == 0:
                    pe.wait_ge(m_scaled_lo, KC)
                if b == 0 and due(PAIR * pair):
                    pe.wait_ge(tT_copied, PAIR * pair)
                if known(pair):
                    span = slice(pair * PAIR * P, (pair + 1) * PAIR * P)
                else:
                    span = bass.ds(pair * (PAIR * P), PAIR * P)
                for d in range(b * KC // 2, (b + 1) * KC // 2):
                    for k in range(KC):
                        for j, (a, h) in enumerate(((m_hi, hT_hi), (m_hi, hT_lo), (m_lo, hT_hi))):
                            mm = pe.matmul(tT_banks[:, d, :], a[:, k, d * P:(d + 1) * P], h[:, k, span],
                                           start=(k == 0 and j == 0), stop=(k == KC - 1 and j == 2))
                if b == 1:
                    mm.then_inc(tT_ready, 1)

            def scores(at, c):
                if c == 0:
                    pe.wait_ge(tT_lo_ready, at.n + 1)
                if due(CHUNKS * at.n + c - 1):
                    pe.wait_ge(scored, CHUNKS * at.n + c - 1)
                if known(at.n) and at.n == 0 and c < 2:
                    pe.wait_ge(v_copied, TILES - 1 + c)
                span = slice(c * CHUNK, (c + 1) * CHUNK)
                for k in range(KC):
                    for j, (a, b) in enumerate(((tT_hi, hT_hi), (tT_hi, hT_lo), (tT_lo, hT_hi))):
                        mm = pe.matmul(z_bank[c % 2][:, :], a[at.u][:, k, :], b[:, k, span],
                                       start=(k == 0 and j == 0), stop=(k == KC - 1 and j == 2))
                mm.then_inc(z_ready, 1)

            def weigh_v(at, c):
                if c == 0 and known(at.n) and at.n == 0:
                    pe.wait_ge(v_lo_ready, TILES)
                    pe.wait_ge(u_copied, 1)
                if c == 0:
                    if due(at.n - 1):
                        pe.wait_ge(o_scaled, at.n - 1)
                if c % BATCH == 0:
                    pe.wait_ge(moved_by_vector, BATCHES * at.n + c // BATCH + 1)
                if c % BATCH == 0:
                    pe.wait_ge(moved_by_scalar, BATCHES * at.n + c // BATCH + 1)
                for b in range(BLOCKS):
                    j = c * BLOCKS + b
                    for s, (part, off) in enumerate(((0, 0), (0, DIM), (1, 0))):
                        mm = pe.matmul(o_bank[at.u][:, :], pT_pair[c // BATCH % 2][:, c % BATCH * BLOCKS + b, :, part],
                                       v_pair[:, j, off:off + DIM],
                                       start=(c == 0 and b == 0 and s == 0),
                                       stop=(c == CHUNKS - 1 and b == BLOCKS - 1 and s == 2))
                mm.then_inc(pv_done, 1)

            def step(at, own=True, prev=True, older=True, fold=True):
                for c in range(CHUNKS):
                    if own:
                        scores(at, c)
                    if c < 2 and at.u == PAIR - 1 and fold:
                        fold_t(at.half + 1, c)
                    if c < BATCH and older:
                        weigh_v(at.back(2), CHUNKS - BATCH + c)
                    if c >= BATCH and prev:
                        weigh_v(at.back(), c - BATCH)

            def group(g, fold=False):
                for j in range(GROUP):
                    at = tile_in(g, j)
                    if not (known(at.n) and at.n <= 1):
                        transpose_h(at)
                    if not (known(at.n) and at.n == 0):
                        project_v(at.back())
                    if fold and j >= GROUP - 2:
                        fold_t(0, j - (GROUP - 2))

            product_m(0)
            product_m(1)
            transpose_h(At(0, 0))
            product_m(2)
            transpose_h(At(0, 1))
            product_m(3)
            pe.wait_ge(bqbk_copied, 1)
            pe.wait_ge(m_copied, 1)
            group(0)
            with pe.Fori(1, GROUPS - 1) as g:
                group(g)
            group(GROUPS - 1, fold=True)
            project_v(tile_in(GROUPS - 1, GROUP - 1))
            step(At(0, 0), prev=False, older=False)
            step(At(0, 1), older=False)
            step(At(1, 0))
            step(At(1, 1))
            with pe.Fori(2, TILES // 2 - 1) as i:
                step(At(i, 0))
                step(At(i, 1))
            last = TILES // 2 - 1
            step(At(last, 0))
            step(At(last, 1), fold=False)
            step(At(last + 1, 0), own=False, fold=False)
            for c in range(CHUNKS - BATCH, CHUNKS):
                weigh_v(At(last, 1), c)

        @block.scalar
        def _(act):
            def flat(ap3):
                return ap3.rearrange("p k n -> p (k n)")

            act.wait_ge(scales_ready, 1)
            for k in range(KC):
                act.wait_ge(wvT_ready, k + 1)
                nc.scalar.activation(wvT_hi[:, k, :], flat(wvT_bank[k]), ACT.Copy, scale=up[0][:, 0:1]
                                     ).then_inc(wvT_scaled_hi, 1)

            def square_root(g):
                act.wait_ge(var_ready, g + 1)
                span = slice(g * GROUP, (g + 1) * GROUP) if known(g) else bass.ds(g * GROUP, GROUP)
                nc.scalar.activation(root[:, span], var_eps[:, span], ACT.Sqrt).then_inc(root_ready, 1)

            square_root(0)
            square_root(1)

            def high_h(at):
                act.wait_ge(hT_ready, at.n + 1)
                nc.scalar.activation(wide(hT_hi, at.n), hT_bank[at.u][:, :, :], ACT.Relu
                                     ).then_inc(hT_hi_ready, 1)

            def copy_v(at):
                act.wait_ge(v_ready, at.n + 1)
                nc.scalar.copy(tile_of(v_pair, at.n, 0, DIM), v_bank[at.u][:, :])
                if due(at.n - 1):
                    act.wait_ge(v_lo_ready, at.n - 1)
                nc.scalar.copy(v_f32[at.u][:, :], v_bank[at.u][:, :]).then_inc(v_copied, 1)

            def high_m(k):
                act.wait_ge(scales_ready, 2)
                nc.scalar.activation(m_hi[:, k, :], m_f32[k], ACT.Copy, scale=up[1][:, 0:1]
                                     ).then_inc(m_scaled_hi, 1)

            def copy_m(d):
                act.wait_ge(m_ready, d + 1)
                nc.scalar.copy(m_f32[d], m_bank[d]).then_inc(m_copied, 1)

            def group(g, roots=True, upper_m=False, lower_m=False):
                for j in range(GROUP):
                    at = tile_in(g, j)
                    if not (known(at.n) and at.n <= 1):
                        high_h(at)
                    if not (known(at.n) and at.n == 0):
                        copy_v(at.back())
                    if upper_m and j == GROUP - 1:
                        high_m(0)
                        high_m(1)
                    if lower_m and j == 0:
                        high_m(2)
                        high_m(3)
                    if j == 0 and roots:
                        square_root(g + 1)

            def high_t(at):
                act.wait_ge(tT_copied, at.n + 1)
                if due(at.n - 1):
                    act.wait_ge(z_ready, CHUNKS * (at.n - 1))
                nc.scalar.copy(tT_hi[at.u][:, :, :], tT_f32[:, :, :]).then_inc(tT_hi_ready, 1)

            def exp(at, c):
                if c == 0:
                    act.wait_ge(max_ready, at.n + 1)
                if due(CHUNKS * at.n + c - 1):
                    act.wait_ge(p_lo_ready, CHUNKS * at.n + c - 1)
                nc.scalar.activation(p_bank[c % 2][:, :], ring[at.u][:, c * CHUNK:(c + 1) * CHUNK], ACT.Exp,
                                     bias=neg_max[at.u][:, 0:1], scale=gain[:, 0:1],
                                     accum_out=sums[at.u][:, c:c + 1]).then_inc(p_ready, 1)

            def high_p(at, c):
                act.wait_ge(p_ready, CHUNKS * at.n + c + 1)
                if due(CHUNKS * at.n + c - 1):
                    act.wait_ge(turned, CHUNKS * at.n + c - 1)
                nc.scalar.mul(p_pair[c % 2][:, :, 0], p_bank[c % 2][:, :], P_SCALE
                              ).then_inc(p_hi_ready, 1)

            def move_p(at, m, share):
                act.wait_ge(turned, CHUNKS * at.n + BATCH * (m + 1))
                if due(CHUNKS * at.n + BATCH * (m - 1)):
                    act.wait_ge(pv_done, CHUNKS * at.n + BATCH * (m - 1))
                quadrant_moves(nc.scalar.copy, m % 2, share).then_inc(moved_by_scalar, 1)

            def step(at, prev=True, fold=True, share=(0, 1)):
                for c in range(CHUNKS):
                    if prev:
                        exp(at.back(), c)
                        high_p(at.back(), c)
                        if c and c % BATCH == 0:
                            move_p(at.back(), c // BATCH - 1, share)
                    if c == 5 and fold:
                        high_t(at.back(-1))
                if prev:
                    move_p(at.back(), BATCHES - 1, share)

            copy_m(0)
            copy_m(1)
            high_h(At(0, 0))
            copy_m(2)
            high_h(At(0, 1))
            copy_m(3)
            group(0, roots=False)
            with act.Fori(1, GROUPS - 2) as g:
                group(g)
            group(GROUPS - 2, upper_m=True)
            group(GROUPS - 1, roots=False, lower_m=True)
            high_t(At(0, 0))
            copy_v(tile_in(GROUPS - 1, GROUP - 1))
            step(At(0, 0), prev=False)
            step(At(0, 1))
            with act.Fori(1, TILES // 2 - 1) as i:
                step(At(i, 0))
                step(At(i, 1))
            last = TILES // 2 - 1
            step(At(last, 0))
            step(At(last, 1), fold=False)
            step(At(last + 1, 0), fold=False, share=(0,))

        @block.vector
        def _(dve):
            v = nc.vector
            seq = [0]

            def link(ins):
                seq[0] += 1
                ins.then_inc(scale_seq, 1)
                dve.wait_ge(scale_seq, seq[0])

            def flat(ap3):
                return ap3.rearrange("p k n -> p (k n)")

            def magnitude(k):
                dve.wait_ge(mag_reduced, k + 1)
                link(v.tensor_reduce(top[k][:, :], mag_all[k][:, :], AX_X, ALU.max))
                link(v.tensor_scalar(top[k][:, :], top[k][:, :], TINY, None, ALU.max))
                link(v.tensor_scalar(up_inv[k][:, :].bitcast(I32), top[k][:, :].bitcast(I32), EXPONENT, None,
                                     ALU.bitwise_and))
                link(v.tensor_scalar(up_inv[k][:, :], up_inv[k][:, :], 1.0 / HEADROOM, None, ALU.mult))
                v.reciprocal(up[k][:, :], up_inv[k][:, :]).then_inc(scales_ready, 1)
                dve.wait_ge(scales_ready, k + 1)

            def row_stats(n, j):
                v.bn_stats(stats[:, j, :], tile_of(rows, n, 0, DIM)).then_inc(stats_ready, 1)

            def aggregate(j):
                v.bn_aggr(mean_var[:, j, :], stats[:, j, :]).then_inc(aggregated, 1)

            def group_span(g):
                return slice(g * GROUP, (g + 1) * GROUP) if known(g) else bass.ds(g * GROUP, GROUP)

            def group_var(g):
                dve.wait_ge(aggregated, GROUP * g + GROUP)
                v.tensor_copy(mean[:, group_span(g)], mean_var[:, :, 0])
                v.tensor_scalar(var_eps[:, group_span(g)], mean_var[:, :, 1], EPS, None, ALU.add
                                ).then_inc(var_ready, 1)

            def group_rstd(g):
                r, span = rstd[:, group_span(g)], group_span(g)
                dve.wait_ge(root_ready, g + 1)
                v.reciprocal(r, root[:, span]).then_inc(inv_root, 1)
                dve.wait_ge(inv_root, g + 1)
                v.tensor_tensor(newton[:, :], r, r, ALU.mult).then_inc(newton_seq, 1)
                dve.wait_ge(newton_seq, 2 * g + 1)
                v.scalar_tensor_tensor(out=newton[:, :], in0=newton[:, :], scalar=-0.5, in1=var_eps[:, span],
                                       op0=ALU.mult, op1=ALU.mult).then_inc(newton_seq, 1)
                dve.wait_ge(newton_seq, 2 * g + 2)
                v.scalar_tensor_tensor(out=r, in0=newton[:, :], scalar=1.5, in1=r,
                                       op0=ALU.add, op1=ALU.mult).then_inc(rstd_ready, 1)

            def normalise(at):
                n = slice(at.n, at.n + 1) if known(at.n) else bass.ds(at.n, 1)
                if due(at.n - 1):
                    dve.wait_ge(hT_ready, at.n - 1)
                if due(at.n - 1):
                    dve.wait_ge(dots_done, at.n - 1)
                v.tensor_scalar(normal[at.u][:, :], tile_of(rows, at.n, 0, DIM), mean[:, n], rstd[:, n],
                                ALU.subtract, ALU.mult).then_inc(normed, 1)

            def largest(dst, src):
                return v.tensor_reduce(dst, src, AX_X, ALU.max, apply_absolute_value=True)

            dve.wait_ge(zeros_ready, 1)
            dve.wait_ge(bias_loaded, 32)
            for k in range(KC):
                v.tensor_scalar(bk_wide[:, k, :], zeros[:, :], b_cols[:, 1, k:k + 1], None, ALU.add
                                ).then_inc(wide_ready, 1)
            dve.wait_ge(wv_loaded, 16)
            for k in range(KC):
                last = largest(mag_v[:, k:k + 1], wv_sb[:, k, :])
            last.then_inc(mag_ready, 1)
            magnitude(0)
            v.tensor_scalar(out_gain[:, :], up_inv[0][:, :], 1.0 / P_SCALE, None, ALU.mult)
            for k in range(KC):
                dve.wait_ge(wvT_scaled_hi, k + 1)
                v.scalar_tensor_tensor(out=wvT_lo[:, k, :], in0=flat(wvT_bank[k]), scalar=up[0][:, 0:1],
                                       in1=wvT_hi[:, k, :], op0=ALU.mult, op1=ALU.subtract
                                       ).then_inc(wvT_scaled_lo, 1)
            def first_stats(g):
                dve.wait_ge(x_loaded, 16 * g + 16)
                for j in range(GROUP):
                    row_stats(GROUP * g + j, j)
                    dve.wait_ge(stats_ready, GROUP * g + j + 1)
                    aggregate(j)
                group_var(g)
                group_rstd(g)

            first_stats(0)
            dve.wait_ge(bk_products_ready, 1)
            dve.wait_ge(rstd_ready, 1)
            normalise(At(0, 0))
            normalise(At(0, 1))
            v.tensor_copy(w_all[:, :], w_bank).then_inc(w_copied, 1)
            v.tensor_copy(bq_bk[:, :], bq_bk_bank).then_inc(bqbk_copied, 1)
            first_stats(1)

            def row_dot(at):
                dve.wait_ge(normed, at.n + 1)
                if due(at.n):
                    dve.wait_ge(dots_done, at.n)
                at_n = slice(at.n, at.n + 1) if known(at.n) else bass.ds(at.n, 1)
                v.scalar_tensor_tensor(out=dot_waste[:, :], in0=normal[at.u][:, :], scalar=0.0,
                                       in1=w_all[:, :], op0=ALU.max, op1=ALU.mult,
                                       accum_out=s_all[:, at_n]).then_inc(dots_done, 1)

            def low_h(at):
                dve.wait_ge(hT_hi_ready, at.n + 1)
                v.scalar_tensor_tensor(out=wide(hT_lo, at.n), in0=hT_bank[at.u][:, :, :], scalar=0.0,
                                       in1=wide(hT_hi, at.n), op0=ALU.max, op1=ALU.subtract
                                       ).then_inc(hT_lo_ready, 1)

            def largest_m(k):
                dve.wait_ge(m_copied, k + 1)
                return largest(mag_m[:, k:k + 1], m_f32[k])

            def largest_u():
                dve.wait_ge(u_ready, KC)
                v.tensor_copy(u_cols[:, :], u_bank).then_inc(u_copied, 1)
                dve.wait_ge(u_copied, 1)
                link(largest(mag_m[:, KC:KC + 1], u_cols[:, :]))
                v.tensor_scalar(mag_m[:, KC:KC + 1], mag_m[:, KC:KC + 1], 1.0 / DIM, None, ALU.mult
                                ).then_inc(mag_ready, 1)

            def scale_m():
                magnitude(1)
                link(v.tensor_scalar(gain[:, :], up_inv[1][:, :], SCALE, None, ALU.mult))
                v.tensor_scalar(neg_gain[:, :], gain[:, :], -1.0, None, ALU.mult)
                link(v.reciprocal(gain_inv[:, :], gain[:, :]))
                v.tensor_scalar(masked_at[:, :], gain_inv[:, :], MASKED, None, ALU.mult)
                v.tensor_scalar(u_cols[:, :], u_cols[:, :], up[1][:, 0:1], None, ALU.mult
                                ).then_inc(u_scaled, 1)

            def low_m(k):
                dve.wait_ge(m_scaled_hi, k + 1)
                v.scalar_tensor_tensor(out=m_lo[:, k, :], in0=m_f32[k], scalar=up[1][:, 0:1],
                                       in1=m_hi[:, k, :], op0=ALU.mult, op1=ALU.subtract
                                       ).then_inc(m_scaled_lo, 1)

            def group(g, stats_too=True, roots=True, of_m=False, own_m=False, more=True):
                for j in range(GROUP):
                    at = tile_in(g, j)
                    if stats_too:
                        if j == 0:
                            dve.wait_ge(x_loaded, 16 * g + 48)
                        row_stats(at.n + 2 * GROUP, j)
                    if (j < GROUP - 1 or more) and not (known(at.n) and at.n == 0):
                        if j == GROUP - 1:
                            dve.wait_ge(rstd_ready, g + 2)
                        normalise(at.back(-1))
                    if not (known(at.n) and at.n <= 1):
                        low_h(at)
                    if stats_too:
                        dve.wait_ge(stats_ready, at.n + 2 * GROUP + 1)
                    row_dot(at)
                    if stats_too:
                        aggregate(j)
                    if j == 1 and roots:
                        group_rstd(g + 1)
                    if of_m and j < 2:
                        largest_m(2 * j)
                        largest_m(2 * j + 1)
                    if of_m and j == 1:
                        largest_u()
                    if of_m and j == GROUP - 1:
                        scale_m()
                    if own_m and j < 2:
                        low_m(2 * j)
                        low_m(2 * j + 1)
                if stats_too:
                    group_var(g + 2)

            def copy_t(at):
                dve.wait_ge(tT_ready, at.half + 1)
                if due(at.n):
                    dve.wait_ge(tT_lo_ready, at.n)
                v.tensor_tensor(tT_f32[:, :, :], tT_banks[:, :, at.u * P:(at.u + 1) * P],
                                u_cols[:, :].unsqueeze(2).to_broadcast([P, KC, P]), ALU.add
                                ).then_inc(tT_copied, 1)

            def copy_s(at):
                col = s_all[:, at.n:at.n + 1] if known(at.n) else s_all[:, bass.ds(at.n, 1)]
                v.tensor_copy(s_tile[at.u][:, :], col).then_inc(s_tile_ready, 1)

            def low_t(at):
                dve.wait_ge(tT_hi_ready, at.n + 1)
                v.tensor_tensor(tT_lo[at.u][:, :, :], tT_f32[:, :, :], tT_hi[at.u][:, :, :], ALU.subtract
                                ).then_inc(tT_lo_ready, 1)

            def mask(at, c):
                g = CHUNKS * at.n + c
                part = ring[at.u][:, c * CHUNK:(c + 1) * CHUNK]
                dve.wait_ge(z_ready, g + 1)
                if c == 0:
                    dve.wait_ge(s_tile_ready, at.n + 1)
                if c % 2 == 0:
                    dve.wait_ge(adj_loaded[at.u][c // 2], 16 * at.half + 16)
                v.scalar_tensor_tensor(out=part, in0=z_bank[c % 2][:, :], scalar=s_tile[at.u][:, 0:1], in1=part,
                                       op0=ALU.add, op1=ALU.mult).then_inc(scored, 1)
                dve.wait_ge(scored, g + 1)
                v.tensor_scalar(penalty[c % 2][:, :], part, 0.0, masked_at[:, 0:1], ALU.is_equal, ALU.mult
                                ).then_inc(penalised, 1)
                dve.wait_ge(scales_ready, 2)
                dve.wait_ge(penalised, g + 1)
                start = LOWEST if c == 0 else run_max[at.u][:, c - 1:c]
                if c:
                    dve.wait_ge(masked, g)
                v.tensor_tensor_reduce(out=part, in0=part, in1=penalty[c % 2][:, :], scale=1.0, scalar=start,
                                       op0=ALU.add, op1=ALU.max, accum_out=run_max[at.u][:, c:c + 1]
                                       ).then_inc(masked, 1)

            def finish_max(at):
                dve.wait_ge(masked, CHUNKS * at.n + CHUNKS)
                v.tensor_scalar(neg_max[at.u][:, :], run_max[at.u][:, CHUNKS - 1:CHUNKS], neg_gain[:, 0:1], None,
                                ALU.mult).then_inc(max_ready, 1)

            def low_p(at, c):
                dve.wait_ge(p_hi_ready, CHUNKS * at.n + c + 1)
                v.scalar_tensor_tensor(out=p_pair[c % 2][:, :, 1], in0=p_bank[c % 2][:, :], scalar=P_SCALE,
                                       in1=p_pair[c % 2][:, :, 0], op0=ALU.mult, op1=ALU.subtract
                                       ).then_inc(p_lo_ready, 1)

            def turn_p(at, c):
                g, m = CHUNKS * at.n + c, BATCHES * at.n + c // BATCH
                dve.wait_ge(p_lo_ready, g + 1)
                if c % BATCH == 0 and due(m - 1):
                    dve.wait_ge(moved_by_scalar, m - 1)
                if c % BATCH == 0 and due(m - 1):
                    dve.wait_ge(moved_by_vector, m - 1)
                span = slice(c % BATCH * CHUNK, (c % BATCH + 1) * CHUNK)
                v.transpose(p_turned[c // BATCH % 2][:, span, :].rearrange("p c s -> p (c s)").bitcast(U32),
                            p_pair[c % 2][:, :, :].rearrange("p c s -> p (c s)").bitcast(U32)
                            ).then_inc(turned, 1)

            def move_p(at, m, share):
                dve.wait_ge(turned, CHUNKS * at.n + BATCH * (m + 1))
                if due(CHUNKS * at.n + BATCH * (m - 1)):
                    dve.wait_ge(pv_done, CHUNKS * at.n + BATCH * (m - 1))
                quadrant_moves(v.tensor_copy, m % 2, share).then_inc(moved_by_vector, 1)

            def row_gain(at):
                dve.wait_ge(p_ready, CHUNKS * at.n + CHUNKS)
                v.tensor_reduce(row_sum[:, :], sums[at.u][:, :], AX_X, ALU.add).then_inc(sum_ready, 1)
                dve.wait_ge(sum_ready, at.n + 1)
                v.reciprocal(row_inv[:, :], row_sum[:, :]).then_inc(inv_ready, 1)
                dve.wait_ge(inv_ready, at.n + 1)
                v.tensor_tensor(row_out[at.u][:, :], row_inv[:, :], out_gain[:, :], ALU.mult
                                ).then_inc(row_out_ready, 1)

            def finish(at):
                if due(16 * at.n):
                    dve.wait_ge(stored, 16 * at.n)
                dve.wait_ge(row_out_ready, at.n + 1)
                dve.wait_ge(pv_done, CHUNKS * at.n + CHUNKS)
                v.scalar_tensor_tensor(out=o_rows[:, :], in0=o_bank[at.u][:, :],
                                       scalar=row_out[at.u][:, 0:1], in1=bv_all[:, :],
                                       op0=ALU.mult, op1=ALU.add).then_inc(o_scaled, 1)
                dve.wait_ge(x_back, 16 * at.n + 16)
                dve.wait_ge(o_scaled, at.n + 1)
                v.scalar_tensor_tensor(out=o_rows[:, :], in0=o_rows[:, :], scalar=0.0,
                                       in1=x_again[:, :], op0=ALU.max, op1=ALU.add
                                       ).then_inc(finished, 1)

            def step(at, own=True, prev=True, fold=True, older=True, share=(2, 3)):
                for c in range(CHUNKS):
                    if c == 3 and fold:
                        copy_t(at.back(-1))
                        copy_s(at.back(-1))
                    if prev:
                        low_p(at.back(), c)
                        turn_p(at.back(), c)
                        if c % BATCH == BATCH - 1:
                            move_p(at.back(), c // BATCH, share)
                    if own:
                        mask(at, c)
                        if c == CHUNKS - 1:
                            finish_max(at)
                    if c == BATCH and own and older:
                        finish(at.back(2))
                    if c == 5 and fold:
                        low_t(at.back(-1))
                if prev:
                    row_gain(at.back())

            dve.wait_ge(w_copied, 1)
            low_h(At(0, 0))
            low_h(At(0, 1))
            group(0, roots=False)
            with dve.Fori(1, GROUPS - 2) as g:
                group(g)
            group(GROUPS - 2, stats_too=False, of_m=True)
            group(GROUPS - 1, stats_too=False, roots=False, own_m=True, more=False)
            dve.wait_ge(u_scaled, 1)
            copy_t(At(0, 0))
            low_t(At(0, 0))
            dve.wait_ge(dots_done, TILES)
            v.tensor_scalar(s_all[:, :], s_all[:, :], bq_bk[:, 0:1], up[1][:, 0:1], ALU.add, ALU.mult
                            ).then_inc(s_all_ready, 1)
            dve.wait_ge(s_all_ready, 1)
            copy_s(At(0, 0))
            dve.wait_ge(bv_loaded, 16)
            dve.wait_ge(v_lo_ready, TILES)
            step(At(0, 0), prev=False, older=False)
            step(At(0, 1), older=False)
            step(At(1, 0))
            step(At(1, 1))
            with dve.Fori(2, TILES // 2 - 1) as i:
                step(At(i, 0))
                step(At(i, 1))
            last = TILES // 2 - 1
            step(At(last, 0))
            step(At(last, 1), fold=False)
            step(At(last + 1, 0), own=False, fold=False, share=(1, 2, 3))
            finish(At(last, 0))
            finish(At(last, 1))


_INS = ["x", "adj", "L0_gnn_W_q", "L0_gnn_b_q", "L0_gnn_W_k", "L0_gnn_b_k", "L0_gnn_W_v", "L0_gnn_b_v"]


def kernel(**inputs):
    import numpy as _np
    import concourse.bacc as _bacc
    from concourse import mybir as _mybir
    from concourse.bass_utils import run_bass_kernel_spmd as _run

    nc = _bacc.Bacc("TRN2", target_bir_lowering=False, num_devices=1)
    arrays, args = {}, []
    for name in _INS:
        a = _np.ascontiguousarray(inputs[name])
        arrays[f"in_{name}"] = a
        args.append(nc.dram_tensor(f"in_{name}", a.shape, _mybir.dt.from_np(a.dtype), kind="ExternalInput").ap())
    out = nc.dram_tensor("out", (NODES, DIM), F32, kind="ExternalOutput").ap()
    adj_preln_attention(nc, *args, out)
    r = _run(nc, [arrays], core_ids=[0])
    return r.results[0]["out"]
```
